# Optimizing a Trainium2 kernel written in Bass

```python
import numpy as np
import jax
import jax.numpy as jnp

def _softmax(x, axis=-1):
    return jax.nn.softmax(x, axis=axis)

def _gelu(x):
    return jax.nn.gelu(x, approximate=True)

def _silu(x):
    return jax.nn.silu(x)

def _sigmoid(x):
    return jax.nn.sigmoid(x)

def _layernorm(x, axis=-1, eps=1e-05):
    m = jnp.mean(x, axis=axis, keepdims=True)
    v = jnp.var(x, axis=axis, keepdims=True)
    return (x - m) / jnp.sqrt(v + eps)

def _scatter_add(tgt, idx, src, axis=0):
    return tgt.at[idx].add(src)

def _segment_sum(src, seg, n):
    return jax.ops.segment_sum(src, seg, n)
kernel_name = 'mk_early_fusion_embed_d2_tok_img256_r4_55a93a'

def setup_inputs(seed: int=0):
    np.random.seed(seed)
    _w = jnp.asarray

    def _rec_inputs():
        import jax
        import jax.numpy as jnp
        _rk = jax.random.key(seed)
        x = -0.000222058 + 0.999998 * jax.random.normal(jax.random.fold_in(_rk, 1), (16, 3, 96, 96), jnp.float32)
        x_txt = jax.random.randint(jax.random.fold_in(_rk, 51), (16, 512), 0, 50257, jnp.int32)
        return (x, x_txt)
    x, x_txt = _rec_inputs()

    def _L0_tok_setup():
        import jax, jax.numpy as jnp
        import numpy as np
        IMAGE_SIZE = 64
        PATCH = 16
        EMBED_DIM = 64
        IN_CH = 3
        BATCH = 128
        IN_DIM = IN_CH * PATCH * PATCH

        def _patchify(x, p):
            B, C, H, Wd = x.shape
            x = x.reshape(B, C, H // p, p, Wd // p, p)
            x = x.transpose(0, 2, 4, 1, 3, 5)
            return x.reshape(B, H // p * (Wd // p), C * p * p)
        key = jax.random.key(seed)
        kx, kw, kb = jax.random.split(key, 3)
        x = jax.random.normal(kx, (BATCH, IN_CH, IMAGE_SIZE, IMAGE_SIZE), dtype=jnp.float32)
        W = jax.random.normal(kw, (EMBED_DIM, IN_DIM), dtype=jnp.float32) * (1.0 / np.sqrt(IN_DIM))
        b = jax.random.normal(kb, (EMBED_DIM,), dtype=jnp.float32) * 0.01
        return {'x': x, 'W': W, 'b': b}
    _L0_tok_all = _L0_tok_setup()
    _L0_tok_in = {k: v for k, v in _L0_tok_all.items() if k in ('W', 'b')}
    del _L0_tok_all

    def _L0_txt_setup():
        import jax, jax.numpy as jnp
        import numpy as np
        VOCAB = 50257
        DIM = 64

        def _positional_table(seq_len, dim, dtype=jnp.float32):
            pos = jnp.arange(seq_len, dtype=dtype)[:, None]
            d = jnp.arange(dim)
            exponent = (d - d % 2).astype(dtype) / dim
            inv_freq = jnp.power(jnp.asarray(10000.0, dtype), -exponent)
            angle = pos * inv_freq
            return jnp.where(d % 2 == 0, jnp.sin(angle), jnp.cos(angle))
        key = jax.random.key(seed)
        k1, k2 = jax.random.split(key)
        x = jax.random.randint(k1, (32, 1024), 0, VOCAB)
        W = jax.random.normal(k2, (VOCAB, DIM), dtype=jnp.float32)
        return {'x': x, 'W': W}
    _L0_txt_all = _L0_txt_setup()
    _L0_txt_in = {k: v for k, v in _L0_txt_all.items() if k in ('W',)}
    del _L0_txt_all

    def _L0_attn_setup():
        import jax, jax.numpy as jnp
        import numpy as np
        B, N, DIM, FFN = (4, 1024, 64, 128)
        EPS = 1e-05

        def _layernorm(x, g, b):
            mu = jnp.mean(x, axis=-1, keepdims=True)
            var = jnp.mean(jnp.square(x - mu), axis=-1, keepdims=True)
            return (x - mu) * jax.lax.rsqrt(var + EPS) * g + b
        key = jax.random.key(seed)
        ks = jax.random.split(key, 10)
        s = 1.0 / np.sqrt(DIM)
        return {'x': jax.random.normal(ks[0], (B, N, DIM), dtype=jnp.float32), 'norm_g': jnp.ones((DIM,), jnp.float32), 'norm_b': jnp.zeros((DIM,), jnp.float32), 'wq': jax.random.normal(ks[1], (DIM, DIM), jnp.float32) * s, 'bq': jnp.zeros((DIM,), jnp.float32), 'wk': jax.random.normal(ks[2], (DIM, DIM), jnp.float32) * s, 'bk': jnp.zeros((DIM,), jnp.float32), 'wv': jax.random.normal(ks[3], (DIM, DIM), jnp.float32) * s, 'bv': jnp.zeros((DIM,), jnp.float32), 'w1': jax.random.normal(ks[4], (DIM, FFN), jnp.float32) * s, 'b1': jnp.zeros((FFN,), jnp.float32), 'w2': jax.random.normal(ks[5], (FFN, DIM), jnp.float32) / np.sqrt(FFN), 'b2': jnp.zeros((DIM,), jnp.float32), 'fnorm_g': jnp.ones((DIM,), jnp.float32), 'fnorm_b': jnp.zeros((DIM,), jnp.float32)}
    _L0_attn_all = _L0_attn_setup()
    _L0_attn_in = {k: v for k, v in _L0_attn_all.items() if k in ('norm_g', 'norm_b', 'wq', 'bq', 'wk', 'bk', 'wv', 'bv', 'w1', 'b1', 'w2', 'b2', 'fnorm_g', 'fnorm_b')}
    del _L0_attn_all

    def _L0_ffn_setup():
        import math
        import jax, jax.numpy as jnp
        import numpy as np
        CAPACITY_FACTOR = 1.25
        key = jax.random.key(seed)
        ks = jax.random.split(key, 5)
        B, L, D, F, E = (8, 2048, 64, 256, 8)
        h = jax.random.normal(ks[0], (B, L, D), dtype=jnp.float32)
        gate_w = jax.random.normal(ks[1], (D, E), dtype=jnp.float32) * 0.02
        gate_b = jnp.zeros((E,), dtype=jnp.float32)
        w1 = jax.random.normal(ks[2], (E, D, F), dtype=jnp.float32) * (1.0 / math.sqrt(D))
        b1 = jnp.zeros((E, F), dtype=jnp.float32)
        w2 = jax.random.normal(ks[3], (E, F, D), dtype=jnp.float32) * (1.0 / math.sqrt(F))
        b2 = jnp.zeros((E, D), dtype=jnp.float32)
        return {'h': h, 'gate_w': gate_w, 'gate_b': gate_b, 'w1': w1, 'b1': b1, 'w2': w2, 'b2': b2}
    _L0_ffn_all = _L0_ffn_setup()
    _L0_ffn_in = {k: v for k, v in _L0_ffn_all.items() if k in ('gate_w', 'gate_b', 'w1', 'b1', 'w2', 'b2')}
    del _L0_ffn_all

    def _L1_attn_setup():
        import jax, jax.numpy as jnp
        import numpy as np
        MIDC = 64
        HEADS = 16
        HEADC = MIDC // HEADS
        EPS = 1e-05

        def _layernorm(x, w, b):
            mean = jnp.mean(x, axis=-1, keepdims=True)
            std = jnp.std(x, axis=-1, keepdims=True, ddof=1)
            return w * (x - mean) / (std + EPS) + b
        key = jax.random.key(seed)
        ks = jax.random.split(key, 3)
        B, HW = (8, 4096)
        x = jax.random.normal(ks[0], (B, HW, MIDC), dtype=jnp.float32)
        W_qkv = jax.random.normal(ks[1], (3 * MIDC, MIDC), dtype=jnp.float32) * 0.02
        b_qkv = jnp.zeros((3 * MIDC,), dtype=jnp.float32)
        kln_w = jnp.ones((HEADS, 1, HEADC), dtype=jnp.float32)
        kln_b = jnp.zeros((HEADS, 1, HEADC), dtype=jnp.float32)
        vln_w = jnp.ones((HEADS, 1, HEADC), dtype=jnp.float32)
        vln_b = jnp.zeros((HEADS, 1, HEADC), dtype=jnp.float32)
        W_proj = jax.random.normal(ks[2], (MIDC, MIDC), dtype=jnp.float32) * 0.02
        b_proj = jnp.zeros((MIDC,), dtype=jnp.float32)
        return {'x': x, 'W_qkv': W_qkv, 'b_qkv': b_qkv, 'kln_w': kln_w, 'kln_b': kln_b, 'vln_w': vln_w, 'vln_b': vln_b, 'W_proj': W_proj, 'b_proj': b_proj}
    _L1_attn_all = _L1_attn_setup()
    _L1_attn_in = {k: v for k, v in _L1_attn_all.items() if k in ('W_qkv', 'b_qkv', 'kln_w', 'kln_b', 'vln_w', 'vln_b', 'W_proj', 'b_proj')}
    del _L1_attn_all

    def _L1_ffn_setup():
        import jax, jax.numpy as jnp
        import numpy as np
        TOP_K = 2
        LN_EPS = 1e-05
        key = jax.random.key(seed)
        ks = jax.random.split(key, 8)
        B, S, D, E, H = (16, 256, 64, 8, 256)
        x = jax.random.normal(ks[0], (B, S, D), dtype=jnp.float32)
        Wr = jax.random.normal(ks[1], (D, E), dtype=jnp.float32) * 0.1
        br = jnp.zeros((E,), dtype=jnp.float32)
        ln_g = jnp.ones((E, D), dtype=jnp.float32)
        ln_b = jnp.zeros((E, D), dtype=jnp.float32)
        W1 = jax.random.normal(ks[2], (E, D, H), dtype=jnp.float32) * (1.0 / np.sqrt(D))
        b1 = jnp.zeros((E, H), dtype=jnp.float32)
        W2 = jax.random.normal(ks[3], (E, H, D), dtype=jnp.float32) * (1.0 / np.sqrt(H))
        b2 = jnp.zeros((E, D), dtype=jnp.float32)
        return {'x': x, 'Wr': Wr, 'br': br, 'ln_g': ln_g, 'ln_b': ln_b, 'W1': W1, 'b1': b1, 'W2': W2, 'b2': b2}
    _L1_ffn_all = _L1_ffn_setup()
    _L1_ffn_in = {k: v for k, v in _L1_ffn_all.items() if k in ('Wr', 'br', 'ln_g', 'ln_b', 'W1', 'b1', 'W2', 'b2')}
    del _L1_ffn_all
    return {'x': x, 'x_txt': x_txt, 'L0_tok_W': _L0_tok_in['W'], 'L0_tok_b': _L0_tok_in['b'], 'L0_txt_W': _L0_txt_in['W'], 'L0_attn_norm_g': _L0_attn_in['norm_g'], 'L0_attn_norm_b': _L0_attn_in['norm_b'], 'L0_attn_wq': _L0_attn_in['wq'], 'L0_attn_bq': _L0_attn_in['bq'], 'L0_attn_wk': _L0_attn_in['wk'], 'L0_attn_bk': _L0_attn_in['bk'], 'L0_attn_wv': _L0_attn_in['wv'], 'L0_attn_bv': _L0_attn_in['bv'], 'L0_attn_w1': _L0_attn_in['w1'], 'L0_attn_b1': _L0_attn_in['b1'], 'L0_attn_w2': _L0_attn_in['w2'], 'L0_attn_b2': _L0_attn_in['b2'], 'L0_attn_fnorm_g': _L0_attn_in['fnorm_g'], 'L0_attn_fnorm_b': _L0_attn_in['fnorm_b'], 'L0_ffn_gate_w': _L0_ffn_in['gate_w'], 'L0_ffn_gate_b': _L0_ffn_in['gate_b'], 'L0_ffn_w1': _L0_ffn_in['w1'], 'L0_ffn_b1': _L0_ffn_in['b1'], 'L0_ffn_w2': _L0_ffn_in['w2'], 'L0_ffn_b2': _L0_ffn_in['b2'], 'L1_attn_W_qkv': _L1_attn_in['W_qkv'], 'L1_attn_b_qkv': _L1_attn_in['b_qkv'], 'L1_attn_kln_w': _L1_attn_in['kln_w'], 'L1_attn_kln_b': _L1_attn_in['kln_b'], 'L1_attn_vln_w': _L1_attn_in['vln_w'], 'L1_attn_vln_b': _L1_attn_in['vln_b'], 'L1_attn_W_proj': _L1_attn_in['W_proj'], 'L1_attn_b_proj': _L1_attn_in['b_proj'], 'L1_ffn_Wr': _L1_ffn_in['Wr'], 'L1_ffn_br': _L1_ffn_in['br'], 'L1_ffn_ln_g': _L1_ffn_in['ln_g'], 'L1_ffn_ln_b': _L1_ffn_in['ln_b'], 'L1_ffn_W1': _L1_ffn_in['W1'], 'L1_ffn_b1': _L1_ffn_in['b1'], 'L1_ffn_W2': _L1_ffn_in['W2'], 'L1_ffn_b2': _L1_ffn_in['b2']}

def reference(x, x_txt, L0_tok_W, L0_tok_b, L0_txt_W, L0_attn_norm_g, L0_attn_norm_b, L0_attn_wq, L0_attn_bq, L0_attn_wk, L0_attn_bk, L0_attn_wv, L0_attn_bv, L0_attn_w1, L0_attn_b1, L0_attn_w2, L0_attn_b2, L0_attn_fnorm_g, L0_attn_fnorm_b, L0_ffn_gate_w, L0_ffn_gate_b, L0_ffn_w1, L0_ffn_b1, L0_ffn_w2, L0_ffn_b2, L1_attn_W_qkv, L1_attn_b_qkv, L1_attn_kln_w, L1_attn_kln_b, L1_attn_vln_w, L1_attn_vln_b, L1_attn_W_proj, L1_attn_b_proj, L1_ffn_Wr, L1_ffn_br, L1_ffn_ln_g, L1_ffn_ln_b, L1_ffn_W1, L1_ffn_b1, L1_ffn_W2, L1_ffn_b2):
    import jax
    import jax.numpy as jnp

    def _L0_tok_ref(x, W, b):
        import jax, jax.numpy as jnp
        import numpy as np
        IMAGE_SIZE = 64
        PATCH = 16
        EMBED_DIM = 64
        IN_CH = 3
        BATCH = 128
        IN_DIM = IN_CH * PATCH * PATCH

        def _patchify(x, p):
            B, C, H, Wd = x.shape
            x = x.reshape(B, C, H // p, p, Wd // p, p)
            x = x.transpose(0, 2, 4, 1, 3, 5)
            return x.reshape(B, H // p * (Wd // p), C * p * p)
        patches = _patchify(x, PATCH)
        return jnp.einsum('bnk,ek->bne', patches, W) + b

    def _L0_txt_ref(x, W):
        import jax, jax.numpy as jnp
        import numpy as np
        VOCAB = 50257
        DIM = 64

        def _positional_table(seq_len, dim, dtype=jnp.float32):
            pos = jnp.arange(seq_len, dtype=dtype)[:, None]
            d = jnp.arange(dim)
            exponent = (d - d % 2).astype(dtype) / dim
            inv_freq = jnp.power(jnp.asarray(10000.0, dtype), -exponent)
            angle = pos * inv_freq
            return jnp.where(d % 2 == 0, jnp.sin(angle), jnp.cos(angle))
        seq_len = x.shape[1]
        pe = _positional_table(seq_len, W.shape[1], W.dtype)
        return W[x] + pe[None, :, :]

    def _L0_attn_ref(x, norm_g, norm_b, wq, bq, wk, bk, wv, bv, w1, b1, w2, b2, fnorm_g, fnorm_b):
        import jax, jax.numpy as jnp
        import numpy as np
        B, N, DIM, FFN = (4, 1024, 64, 128)
        EPS = 1e-05

        def _layernorm(x, g, b):
            mu = jnp.mean(x, axis=-1, keepdims=True)
            var = jnp.mean(jnp.square(x - mu), axis=-1, keepdims=True)
            return (x - mu) * jax.lax.rsqrt(var + EPS) * g + b
        scale = DIM ** (-0.5)
        h = _layernorm(x, norm_g, norm_b)
        Q = h @ wq + bq
        K = h @ wk + bk
        V = h @ wv + bv
        scores = jnp.einsum('bnd,bmd->bnm', Q, K) * scale
        attn = jax.nn.relu(scores)
        R = x + jnp.einsum('bnm,bmd->bnd', attn, V)
        ffn_out = jax.nn.relu(R @ w1 + b1) @ w2 + b2
        return _layernorm(R + ffn_out, fnorm_g, fnorm_b)

    def _L0_ffn_ref(h, gate_w, gate_b, w1, b1, w2, b2):
        import math
        import jax, jax.numpy as jnp
        import numpy as np
        CAPACITY_FACTOR = 1.25
        B, L, D = h.shape
        E = gate_w.shape[1]
        T = B * L
        C = max(1, math.ceil(CAPACITY_FACTOR * T / E))
        x = h.reshape(T, D)
        logits = x @ gate_w + gate_b
        probs = jax.nn.softmax(logits, axis=-1)
        idx = jnp.argmax(probs, axis=-1)
        prb = jnp.take_along_axis(probs, idx[:, None], axis=1)[:, 0]
        one_hot = jax.nn.one_hot(idx, E, dtype=jnp.float32)
        pos = (jnp.cumsum(one_hot, axis=0) * one_hot).sum(-1).astype(jnp.int32) - 1
        kept = pos < C
        pos_safe = jnp.where(kept, pos, C)
        buf = jnp.zeros((E, C, D), dtype=h.dtype).at[idx, pos_safe].set(x, mode='drop')
        hmid = jax.nn.relu(jnp.einsum('ecd,edf->ecf', buf, w1) + b1[:, None, :])
        ybuf = jnp.einsum('ecf,efd->ecd', hmid, w2) + b2[:, None, :]
        pos_g = jnp.minimum(pos, C - 1)
        y_tok = ybuf[idx, pos_g] * (prb * kept)[:, None]
        y = y_tok.reshape(B, L, D)
        y = jnp.nan_to_num(y, nan=0.0, posinf=10000.0, neginf=-10000.0)
        return y

    def _L1_attn_ref(x, W_qkv, b_qkv, kln_w, kln_b, vln_w, vln_b, W_proj, b_proj):
        import jax, jax.numpy as jnp
        import numpy as np
        MIDC = 64
        HEADS = 16
        HEADC = MIDC // HEADS
        EPS = 1e-05

        def _layernorm(x, w, b):
            mean = jnp.mean(x, axis=-1, keepdims=True)
            std = jnp.std(x, axis=-1, keepdims=True, ddof=1)
            return w * (x - mean) / (std + EPS) + b
        B, HW, C = x.shape
        bias = x
        qkv = jnp.einsum('bnc,oc->bno', x, W_qkv) + b_qkv
        qkv = qkv.reshape(B, HW, HEADS, 3 * HEADC).transpose(0, 2, 1, 3)
        q, k, v = jnp.split(qkv, 3, axis=-1)
        k = _layernorm(k, kln_w, kln_b)
        v = _layernorm(v, vln_w, vln_b)
        kv = jnp.einsum('bhnd,bhne->bhde', k, v) / HW
        out = jnp.einsum('bhnd,bhde->bhne', q, kv)
        out = out.transpose(0, 2, 1, 3).reshape(B, HW, C)
        ret = out + bias
        proj = jnp.einsum('bnc,oc->bno', ret, W_proj) + b_proj
        return jax.nn.gelu(proj, approximate=False) + bias

    def _L1_ffn_ref(x, Wr, br, ln_g, ln_b, W1, b1, W2, b2):
        import jax, jax.numpy as jnp
        import numpy as np
        TOP_K = 2
        LN_EPS = 1e-05
        B, S, D = x.shape
        N = B * S
        xt = x.reshape(N, D)
        logits = xt @ Wr + br
        probs = jax.nn.softmax(logits, axis=-1)
        top_p, top_idx = jax.lax.top_k(probs, TOP_K)
        weights = top_p / top_p.sum(axis=-1, keepdims=True)
        mu = xt.mean(axis=-1, keepdims=True)
        var = ((xt - mu) ** 2).mean(axis=-1, keepdims=True)
        xn = (xt - mu) * jax.lax.rsqrt(var + LN_EPS)
        xe = xn[None, :, :] * ln_g[:, None, :] + ln_b[:, None, :]
        h = jax.nn.gelu(jnp.einsum('end,edh->enh', xe, W1) + b1[:, None, :], approximate=False)
        y = jnp.einsum('enh,ehd->end', h, W2) + b2[:, None, :]
        y_tok = jnp.transpose(y, (1, 0, 2))
        sel = jnp.take_along_axis(y_tok, top_idx[:, :, None], axis=1)
        out = (weights[:, :, None] * sel).sum(axis=1)
        return out.reshape(B, S, D)
    h = _L0_tok_ref(x, L0_tok_W, L0_tok_b)
    h = jnp.concatenate([h, _L0_txt_ref(x_txt, L0_txt_W)], axis=1)
    h = h + _L0_attn_ref(_layernorm(h, axis=-1), L0_attn_norm_g, L0_attn_norm_b, L0_attn_wq, L0_attn_bq, L0_attn_wk, L0_attn_bk, L0_attn_wv, L0_attn_bv, L0_attn_w1, L0_attn_b1, L0_attn_w2, L0_attn_b2, L0_attn_fnorm_g, L0_attn_fnorm_b)
    h = h + _L0_ffn_ref(_layernorm(h, axis=-1), L0_ffn_gate_w, L0_ffn_gate_b, L0_ffn_w1, L0_ffn_b1, L0_ffn_w2, L0_ffn_b2)
    h = h + _L1_attn_ref(_layernorm(h, axis=-1), L1_attn_W_qkv, L1_attn_b_qkv, L1_attn_kln_w, L1_attn_kln_b, L1_attn_vln_w, L1_attn_vln_b, L1_attn_W_proj, L1_attn_b_proj)
    h = h + _L1_ffn_ref(_layernorm(h, axis=-1), L1_ffn_Wr, L1_ffn_br, L1_ffn_ln_g, L1_ffn_ln_b, L1_ffn_W1, L1_ffn_b1, L1_ffn_W2, L1_ffn_b2)
    return h

_drawn_inputs = setup_inputs


def setup_inputs(seed=0):
    import zlib

    import numpy as np

    out = dict(_drawn_inputs(seed))
    spreads = {'L0_attn_norm_g': (1.0, 0.2),
     'L0_attn_norm_b': (0.0, 0.1),
     'L0_attn_bq': (0.0, 0.1),
     'L0_attn_bk': (0.0, 0.368),
     'L0_attn_bv': (0.0, 0.1),
     'L0_attn_b1': (0.0, 0.8),
     'L0_attn_b2': (0.0, 0.8),
     'L0_attn_fnorm_g': (1.0, 0.2),
     'L0_attn_fnorm_b': (0.0, 0.1),
     'L0_ffn_gate_b': (0.0, 0.1),
     'L0_ffn_b1': (0.0, 0.8),
     'L0_ffn_b2': (0.0, 0.712),
     'L1_attn_b_qkv': (0.0, 0.8),
     'L1_attn_kln_w': (1.0, 0.6),
     'L1_attn_kln_b': (0.0, 0.8),
     'L1_attn_vln_w': (1.0, 0.6),
     'L1_attn_vln_b': (0.0, 0.8),
     'L1_attn_b_proj': (0.0, 0.283),
     'L1_ffn_br': (0.0, 0.1),
     'L1_ffn_ln_g': (1.0, 0.2),
     'L1_ffn_ln_b': (0.0, 0.43),
     'L1_ffn_b1': (0.0, 0.443),
     'L1_ffn_b2': (0.0, 0.287)}
    factors = {'L0_tok_b': 8.0, 'L1_attn_W_qkv': 5.909}
    for name, (base, spread) in spreads.items():
        noise = np.random.default_rng([zlib.crc32(name.encode()), seed]).standard_normal(out[name].shape)
        drawn = base * np.exp(spread * noise) if base else spread * noise
        out[name] = jnp.asarray(drawn.astype(out[name].dtype))
    for name, factor in factors.items():
        out[name] = (out[name] * factor).astype(out[name].dtype)
    return out
```

```python
from contextlib import ExitStack

import concourse.bass as bass
from concourse import mybir

F32 = mybir.dt.float32
F32R = mybir.dt.float32r
BF16 = mybir.dt.bfloat16
I32 = mybir.dt.int32
ALU = mybir.AluOpType
ACT = mybir.ActivationFunctionType
AX = mybir.AxisListType.X

P = 128
NB, N_IMG, N_TXT, D = 16, 36, 512, 64
N = N_IMG + N_TXT
SLOTS = 5
IMG = 4
TXT = N_TXT // P
NPAD = SLOTS * P
KC = 6
E = 8
F_ATTN = 128
F_MOE = 256
J = F_MOE // P
CAP = -(-5 * NB * N // (4 * E))
ET = -(-CAP // P)
CP = ET * P
DROPPED = 1.0e6
EPS = 1e-5
SCALE = D ** -0.5
HALF = N // 2
LEFT = 2 * P
RIGHT = N - LEFT
HC = 4
FMAX = 3.4028234663852886e38

PER = dict(norm1a=11, norm1b=6, qk_low=3, vals=1, resid=4, norm2a=12, norm2b=6, norm3a=10, norm3b=5, gate=7, place=7,
           mixed=17, norm4=5, kvnorm=3, fold=3, resid2=12, norm5=6, route_a=10, route_b=6)


class Steps:

    def __init__(self, engine, sem, name, b):
        self.engine, self.sem, self.name = engine, sem, name
        self.n, self.end = b * PER[name], (b + 1) * PER[name]

    def __call__(self, ins):
        ins.then_inc(self.sem, 1)
        self.n += 1

    def sync(self):
        self.engine.wait_ge(self.sem, self.n)

    def close(self):
        assert self.n == self.end, (self.name, self.n - self.end + PER[self.name])



class Banks:

    def __init__(self):
        self.reader = {}

    def take(self, pe, banks, sem, value):
        before = {self.reader[k] for k in banks if k in self.reader}
        for s, v in before:
            pe.wait_ge(s, v)
        for k in banks:
            self.reader[k] = (sem, value)


def early_fusion_kernel(nc, i, out):
    with ExitStack() as ctx:
        def sb(name, shape, dt=F32):
            return ctx.enter_context(nc.sbuf_tensor(name, shape, dt))

        def pair(name, shape, dt=F32, depth=2):
            return [sb(f"{name}{k}", shape, dt) for k in range(depth)]

        sems = {}

        def sem(name):
            if name not in sems:
                sems[name] = ctx.enter_context(nc.semaphore(name))
            return sems[name]

        psum = ctx.enter_context(nc.psum_tensor("psum", [P, 8 * 512], F32))

        def bank(k, n=1):
            return psum[:, 512 * k:512 * (k + n)]

        slots_buf = nc.dram_tensor("slots_buf", [E * CP, 2 * D], F32, kind="Internal").ap()
        expert_out = nc.dram_tensor("expert_out", [E * CP, D], F32, kind="Internal").ap()

        H = sb("H", [P, NB, SLOTS, D])
        X = sb("X", [P, NB, SLOTS, D])
        scratch = sb("scratch", [P, 5120])
        early_x = X[:].rearrange("p b s c -> p (b s c)")
        patches = early_x[:, 0:KC * NB * N_IMG].rearrange("p (k n) -> p k n", k=KC)
        ew1 = scratch[:, 0:E * F_MOE]
        fw1 = scratch[:, E * F_MOE:2 * E * F_MOE]
        w = {}
        for name in i:
            if name not in ("table", "patches", "ew1", "fw1"):
                w[name] = sb("w_" + name, list(i[name].shape), i[name].dtype)
        ident = w["ident"]
        tri_b, ones_b = sb("tri_b", [P, P], BF16), sb("ones_b", [P, P], BF16)
        eps_t = sb("eps_t", [P, 2])
        split = {}
        for name, cols in (("wq", P), ("wk", P), ("wv", D), ("w1", F_ATTN), ("gw", E), ("wr", E), ("wkv", 2 * D),
                           ("ew1", E * F_MOE), ("fw1", E * F_MOE)):
            split[name] = (sb(name + "_hi", [P, cols], F32R), sb(name + "_lo", [P, cols], F32R))
        bq, bk, bv = sb("bq", [P, 1]), sb("bk", [P, 1]), sb("bv", [P, D])
        fb1 = sb("fb1", [P, E * J])
        ctr_w, ctr_b = sb("ctr_w", [P, 2 * D // HC]), sb("ctr_b", [P, 2 * D // HC])
        ak, av = sb("ak", [D + 1, D]), sb("av", [D + 1, D])
        img_t = scratch[0:D, 2 * E * F_MOE:2 * E * F_MOE + NB * N_IMG]
        gap = sb("gap", [P, NB, SLOTS, E])
        slot_f, slot_i = sb("slot_f", [P, NB, SLOTS]), sb("slot_i", [P, NB, SLOTS], I32)
        top_w, kept = sb("top_w", [P, NB, SLOTS]), sb("kept", [P, NB, SLOTS])
        carry = sb("carry", [P, E])

        emb = pair("emb", [P, TXT, D])
        stats = sb("stats", [P, SLOTS, 6])
        mv1, mv2, mv3 = (pair(f"mv{k}_", [P, SLOTS, 2]) for k in (1, 2, 3))
        sd1 = pair("sd1_", [P, 2, SLOTS])
        sd2, sd3 = pair("sd2_", [P, SLOTS]), pair("sd3_", [P, SLOTS])
        rs = sb("rs", [P, 2, SLOTS])
        zt, xt = sb("zt", [P, SLOTS, D]), sb("xt", [P, SLOTS, D])
        uu = pair("uu", [P, SLOTS, D])
        hl1, hl2 = pair("hl1_", [P, SLOTS, 2 * D]), pair("hl2_", [P, SLOTS, 2 * D])
        hl3 = pair("hl3_", [P, SLOTS, 2 * D], depth=4)
        xs1, xs2, xs3 = (pair(f"xs{k}_", [P, NPAD], F32R) for k in (1, 2, 3))
        qst = pair("qst", [P, N], F32R)
        kh, kl = pair("kh", [P, NPAD], F32R), pair("kl", [P, NPAD], F32R)
        vv = pair("vv", [P, SLOTS, D])
        prob_t = sb("prob", [P, SLOTS, N])
        prob = [prob_t[:, s, :] for s in range(SLOTS)]
        zeros = sb("zeros", [P, 2 * D])
        ot, yt = pair("ot", [P, RIGHT]), pair("yt", [P, RIGHT])
        rr = pair("rr", [P, SLOTS, D])
        ff = pair("ff", [P, N])
        lg, mx = sb("lg", [P, SLOTS, E]), sb("mx", [P, SLOTS])
        eq, oh = sb("eq", [P, SLOTS, E]), pair("oh", [P, SLOTS + 1, E])
        oh_b = pair("oh_b", [P, SLOTS + 1, E], BF16)
        pl, ov = sb("pl", [P, SLOTS, E]), sb("ov", [P, SLOTS, E])
        def cut(start, k, shape):
            size = shape[0] * shape[1]
            return scratch[:, start + k * size:start + (k + 1) * size].rearrange("p (a c) -> p a c", a=shape[0])

        xl = [cut(0, k, (ET, 2 * D)) for k in range(2)]
        yo = [cut(2 * ET * 2 * D, k, (ET, D)) for k in range(2)]
        by = [scratch[:, 6 * ET * D + k * LEFT:6 * ET * D + (k + 1) * LEFT] for k in range(2)]
        bx = [q[:, 0:512] for q in qst]
        bg = [prob_t[:].rearrange("p s n -> p (s n)")[:, k * J * 512:(k + 1) * J * 512].rearrange("p (j n) -> p j n", j=J) for k in range(2)]

        def bc(a, n):
            return a.unsqueeze(2).to_broadcast([a.shape[0], a.shape[1], n])

        def bs(a, k):
            return a.unsqueeze(1).to_broadcast([a.shape[0], k, a.shape[1]])

        def halves(k):
            return bank(k, 2).rearrange("p (h n) -> p h n", h=2)[:, :, 0:HALF]

        def turned(k):
            return bank(k)[:, 0:4 * D].rearrange("p (r g c) -> p r g c", r=2, g=2)

        def by_pairs(a):
            return a[:, 0:TXT, :].rearrange("p (g r) c -> p r g c", g=2)

        TURN, WIDE, SCORE, MIX, LOW = (0, 1), (2, 3), (4, 5), (6,), (7,)
        LAG = dict(gather=0, norm1=1, qkv=2, attn=3, resid=4, ffn2=5, gate=6, scatter=7)
        STEPS = NB + 7

        def at(step, stage):
            b = step - LAG[stage]
            return b if 0 <= b < NB else None

        block = ctx.enter_context(nc.Block())
        loads = [n for n in w if n != "ids"]
        LOADED = 16 * (len(loads) + 2)
        B_STEPS = [(e, c) for e in range(E) for c in range(0, ET, 4)]
        NU = len(B_STEPS)
        UE = NU // E

        def piece(start, *shape):
            size = 1
            for k in shape:
                size *= k
            v = scratch[:, start:start + size]
            if len(shape) == 2:
                return v.rearrange("p (a c) -> p a c", a=shape[0])
            if len(shape) == 3:
                return v.rearrange("p (a k c) -> p a k c", a=shape[0], k=shape[1])
            return v

        hid = [piece(k * RIGHT, RIGHT) for k in range(8)]
        at0 = 8 * RIGHT
        kvn = piece(at0, SLOTS, 2, D + 1)
        at0 += SLOTS * 2 * (D + 1)
        acc = piece(at0, SLOTS, 2, D)
        at0 += SLOTS * 2 * D
        tmp = [piece(at0 + k * 3 * P, 3, 2, D) for k in range(2)]
        at0 += 2 * 3 * P
        ssq, ksd, krs = (piece(at0 + k * SLOTS * 32, SLOTS, 32) for k in range(3))
        yg, kvt, ksq, ysb = uu, hl2[0], hl2[1], yt
        gram_s, p1_s, kv_s, a_s, fold_b = ff[0][0:D + 1, 0:D + 1], ff[0][0:D + 1, 128:128 + D], ff[0][0:D, 256:256 + D], ff[0][0:D, 384:384 + D + 1], ff[1][:, 0:D]
        fold_w = (kh[0][:, 0:D], kl[0][:, 0:D])
        pre, gel = vv[0], vv[1]
        good = rr[0]
        ratio = pair("ratio", [P, SLOTS])
        w8 = pair("w8_", [P, SLOTS, E])
        oh2, ex, qq = sb("oh2_", [P, SLOTS, E]), sb("ex", [P, SLOTS]), sb("qq", [P, SLOTS])
        euler = sb("euler", [P, SLOTS])
        POS = 8
        LAG2 = dict(gather=0, mixed=1, kv=2, fold=3, norm5=4, moe=5)
        STEPS2 = NB + LAG2["moe"] + 1
        PARTS = ((0, LEFT, 0, 2), (LEFT, N, 2, SLOTS))

        def at2(step, stage):
            b = step - LAG2[stage]
            return b if 0 <= b < NB else None

        def up_bank(m):
            return 2 + m % 3

        def unit(n):
            b, k = divmod(n, POS)
            return (b,) + divmod(k, E // 2)

        def wide(k):
            return bank(k, 2)[:, 0:SLOTS * P].rearrange("p (s c) -> p s c", s=SLOTS)

        def groups(a):
            return a.rearrange("p s (g c) -> p s g c", c=HC)

        def outputs(sp):
            for b in range(NB):
                sp.wait_ge(sem("finish"), 4 * (b + 1))
                sp.dma_start(out[b, N_IMG:N, :].rearrange("(t p) c -> p t c", p=P), H[:, b, 0:TXT, :]).then_inc(sem("out_stored"), 16)
                sp.dma_start(out[b, 0:N_IMG, :], H[0:N_IMG, b, IMG, :]).then_inc(sem("out_stored"), 16)
            sp.wait_ge(sem("out_stored"), 32 * NB)

        def pool_second(pool):
            for k in range(2):
                pool.wait_ge(sem(f"expert_out{k}"), 16 * E // 2)
            pool.memset(euler[:], 2.718281828459045).then_inc(sem("euler"), 1)
            pool.wait_ge(sem("euler"), 1)
            pool.wait_ge(sem("norm2a"), NB * PER["norm2a"])
            pool.wait_ge(sem("norm2b"), NB * PER["norm2b"])

            def gather_y(b):
                if b >= 2:
                    pool.wait_ge(sem("mixed"), (b - 1) * PER["mixed"])
                for s in range(SLOTS):
                    rows = P if s < TXT else N_IMG
                    pool.indirect_dma_start(yg[b % 2][0:rows, s, :], None, expert_out, bass.IndirectOffsetOnAxis(slot_i[0:rows, b, s:s + 1], 0),
                                            bounds_check=E * CP - 1, oob_is_err=False).then_inc(sem(f"y_in{b % 2}"), 16)

            def second_share(b):
                pool.wait_ge(sem("route_a"), (b + 1) * PER["route_a"])
                if b >= 1:
                    pool.wait_ge(sem("route_b"), b * PER["route_b"])
                pool.tensor_tensor(ex[:], euler[:], mx[:], ALU.pow).then_inc(sem("share"), 1)

            for step in range(STEPS2):
                for stage, f in (("gather", gather_y), ("norm5", second_share)):
                    if (b := at2(step, stage)) is not None:
                        f(b)

        def pe_second(pe):
            NARROW, DOWN, BACK = (5,), (6,), (7,)

            def t4(b):
                banks.take(pe, (0, 1), sem("xs4"), b + 1)
                pe.wait_ge(sem("norm4"), (b + 1) * PER["norm4"])
                turn(pe, hl1[b % 2], 0).then_inc(sem("t4"), 1)

            def kv(b):
                banks.take(pe, (0, 1), sem("kv_b"), b + 1)
                pe.wait_ge(sem("xs4"), b + 1)
                tokens_by(pe, wide(0), xs1[b % 2], split["wkv"], slice(0, 2 * D)).then_inc(sem("kv_prod"), 1)

            def gram(b):
                banks.take(pe, NARROW, sem("gram_s"), b + 1)
                pe.wait_ge(sem("kvnorm"), (b + 1) * PER["kvnorm"])
                for s in range(SLOTS):
                    rows = P if s < TXT else N_IMG
                    last = pe.matmul(bank(5)[0:D + 1, 0:D + 1], kvn[0:rows, s, 0, :], kvn[0:rows, s, 1, :], start=(s == 0), stop=(s == IMG))
                last.then_inc(sem("gram"), 1)

            def gains_k(b):
                banks.take(pe, NARROW, sem("p1_s"), b + 1)
                pe.wait_ge(sem("gram_s"), b + 1)
                pe.matmul(bank(5)[0:D + 1, 0:D], gram_s, ak[:], start=True, stop=True).then_inc(sem("p1"), 1)

            def gains_v(b):
                banks.take(pe, NARROW, sem("kv_s"), b + 1)
                pe.wait_ge(sem("p1_s"), b + 1)
                pe.matmul(bank(5)[0:D, 0:D], p1_s, av[:], start=True, stop=True).then_inc(sem("p2"), 1)

            def by_q(b):
                banks.take(pe, NARROW, sem("a_s"), b + 1)
                pe.wait_ge(sem("kv_s"), b + 1)
                pe.matmul(bank(5)[0:D, 0:D + 1], kv_s, w["l1_wq"][:], start=True, stop=True).then_inc(sem("p3"), 1)

            def by_proj(b):
                banks.take(pe, NARROW, sem("fold"), (b + 1) * PER["fold"])
                pe.wait_ge(sem("a_s"), b + 1)
                for h in range(2):
                    pe.matmul(bank(5)[h * D:(h + 1) * D, 0:D], a_s[:, 0:D], w["wp"][:], start=True, stop=True)
                pe.matmul(bank(5)[:, D:2 * D], a_s[:, D:D + 1].to_broadcast([D, P]), w["wp"][:], start=True, stop=True).then_inc(sem("p4"), 1)

            def proj(b):
                banks.take(pe, (1,), sem("pre"), b + 1)
                pe.wait_ge(sem("fold"), (b + 1) * PER["fold"])
                tokens_by(pe, bank(1)[:, 0:SLOTS * D].rearrange("p (s c) -> p s c", s=SLOTS), xs1[b % 2], fold_w, slice(0, D)).then_inc(sem("proj"), 1)

            def t5(b):
                banks.take(pe, (0, 1), sem("xs5"), b + 1)
                pe.wait_ge(sem("norm5"), (b + 1) * PER["norm5"])
                turn(pe, hl3[b % 2], 0).then_inc(sem("t5"), 1)

            def route(b):
                banks.take(pe, (1,), sem("route_a"), b * PER["route_a"] + 1)
                pe.wait_ge(sem("xs5"), b + 1)
                tokens_by(pe, bank(1)[:, 0:SLOTS * E].rearrange("p (s e) -> p s e", s=SLOTS), xs2[b % 2], split["wr"], slice(0, E)).then_inc(sem("route_prod"), 1)

            def up(n, half):
                b, side, p = unit(n)
                a, z, _, _ = PARTS[side]
                if n % POS == 0 and half == 0:
                    pe.wait_ge(sem("xs5"), b + 1)
                for k in (2 * half, 2 * half + 1):
                    j, e = k // 2, 2 * p + k % 2
                    m = up_bank(4 * n + k)
                    banks.take(pe, (m,), sem("gelu"), 4 * n + k + 1)
                    two(pe, bank(m)[:, 0:z - a], split["fw1"], xs2[b % 2][:, a:z], slice((e * J + j) * P, (e * J + j + 1) * P)).then_inc(sem("up"), 1)

            def down(n):
                b, side, p = unit(n)
                a, z, _, _ = PARTS[side]
                banks.take(pe, DOWN, sem("ysb"), n + 1)
                for j in range(J):
                    pe.wait_ge(sem("gelu"), 4 * n + 2 * j + 2)
                    for h in range(2):
                        last = pe.matmul(bank(6)[h * D:(h + 1) * D, 0:z - a], w["fw2"][:, (2 * p + h) * J + j, :], hid[(4 * n + 2 * j + h) % 8][:, 0:z - a],
                                         start=(j == 0), stop=(j == J - 1))
                last.then_inc(sem("down"), 1)

            def back(n):
                b, side, p = unit(n)
                _, _, s0, s1 = PARTS[side]
                banks.take(pe, BACK, sem("weigh"), 2 * n + 1)
                pe.wait_ge(sem("ysb"), n + 1)
                for s in range(s0, s1):
                    rows = P if s < TXT else N_IMG
                    k = (s - s0) * P
                    last = pe.transpose(bank(7)[0:rows, k:k + P], ysb[n % 2][:, k:k + rows], ident[:])
                last.then_inc(sem("back"), 1)

            for step in range(STEPS2):
                K, F, W5 = (at2(step, k) for k in ("kv", "fold", "norm5"))
                for pos in range(POS):
                    n = (step - LAG2["moe"]) * POS + pos
                    if 0 <= n < NB * POS:
                        up(n, 0)
                    if 0 <= n - 2 < NB * POS:
                        back(n - 2)
                    for stage, when, f in PE_ORDER:
                        if when == pos and at2(step, stage) is not None:
                            {"t5": t5, "gram": gram, "gains_k": gains_k, "t4": t4, "gains_v": gains_v, "route": route, "by_q": by_q, "kv": kv,
                             "by_proj": by_proj, "proj": proj}[f](at2(step, stage))
                    if 0 <= n < NB * POS:
                        up(n, 1)
                    if 0 <= n - 1 < NB * POS:
                        down(n - 1)

        def act_second(act):
            def roots4(b):
                act.wait_ge(sem("mixed"), (b + 1) * PER["mixed"])
                if b >= 2:
                    act.wait_ge(sem("norm4"), (b - 2) * PER["norm4"] + 1)
                act.activation(sd2[b % 2][:], mv1[b % 2][:, :, 1], ACT.Sqrt, bias=eps_t[:, 0:1]).then_inc(sem("roots4"), 1)

            def roots_kv(b):
                act.wait_ge(sem("ssq"), b + 1)
                act.activation(ksd, ssq, ACT.Sqrt, scale=1.0 / (HC - 1)).then_inc(sem("roots_kv"), 1)

            def roots5(b):
                act.wait_ge(sem("resid2"), (b + 1) * PER["resid2"])
                if b >= 2:
                    act.wait_ge(sem("norm5"), (b - 1) * PER["norm5"])
                act.activation(sd1[b % 2][:, 0, :], mv2[b % 2][:, :, 1], ACT.Sqrt, bias=eps_t[:, 0:1])
                act.activation(sd1[b % 2][:, 1, :], mv2[b % 2][:, :, 1], ACT.Sqrt, bias=eps_t[:, 1:2], scale=1.0 + EPS).then_inc(sem("roots5"), 1)

            def stack4(b):
                act.wait_ge(sem("t4"), b + 1)
                if b >= 2:
                    act.wait_ge(sem("proj"), b - 1)
                act.activation(xs1[b % 2][:, 0:N], bank(0, 2)[:, 0:N], ACT.Identity).then_inc(sem("xs4"), 1)

            def square(b):
                act.wait_ge(sem("kv_b"), b + 1)
                if b >= 1:
                    act.wait_ge(sem("ssq"), b)
                act.activation(ksq[:], kvt[:], ACT.Square).then_inc(sem("ksq"), 1)

            def gelu_proj(b):
                act.wait_ge(sem("pre"), b + 1)
                if b >= 1:
                    act.wait_ge(sem("resid2"), (b - 1) * PER["resid2"] + 1)
                act.activation(gel[:], pre[:], ACT.Gelu).then_inc(sem("gelu_proj"), 1)

            def stack5(b):
                act.wait_ge(sem("t5"), b + 1)
                if b >= 2:
                    act.wait_ge(sem("up"), 4 * POS * (b - 1))
                act.activation(xs2[b % 2][:, 0:N], bank(0, 2)[:, 0:N], ACT.Identity).then_inc(sem("xs5"), 1)

            def gelu(n, half):
                b, side, p = unit(n)
                a, z, _, _ = PARTS[side]
                for k in (2 * half, 2 * half + 1):
                    j, e = k // 2, 2 * p + k % 2
                    m = 4 * n + k
                    act.wait_ge(sem("up"), m + 1)
                    if m >= 8:
                        act.wait_ge(sem("down"), n - 1)
                    act.activation(hid[m % 8][:, 0:z - a], bank(up_bank(m))[:, 0:z - a], ACT.Gelu, bias=fb1[:, e * J + j:e * J + j + 1]).then_inc(sem("gelu"), 1)

            def add_b2(n):
                b, side, p = unit(n)
                a, z, _, _ = PARTS[side]
                act.wait_ge(sem("down"), n + 1)
                if n >= 2:
                    act.wait_ge(sem("back"), n - 1)
                act.activation(ysb[n % 2][:, 0:z - a], bank(6)[:, 0:z - a], ACT.Identity, bias=w["fb2"][:, p:p + 1]).then_inc(sem("ysb"), 1)

            for k in range(2):
                act.wait_ge(sem(f"expert_out{k}"), 16 * E // 2)
            for step in range(STEPS2):
                for pos in range(POS):
                    n = (step - LAG2["moe"]) * POS + pos
                    if 0 <= n < NB * POS:
                        gelu(n, 0)
                    for stage, when, f in ACT_ORDER:
                        if when == pos and at2(step, stage) is not None:
                            {"roots4": roots4, "roots_kv": roots_kv, "roots5": roots5, "stack4": stack4, "square": square, "gelu_proj": gelu_proj,
                             "stack5": stack5}[f](at2(step, stage))
                    if 0 <= n < NB * POS:
                        gelu(n, 1)
                    if 0 <= n - 1 < NB * POS:
                        add_b2(n - 1)

        def dve_second(dve):
            for k in range(2):
                dve.wait_ge(sem(f"expert_out{k}"), 16 * E // 2)
            dve.memset(kvn[:, :, :, D:D + 1], 1.0).then_inc(sem("kvn_ones"), 1)
            dve.wait_ge(sem("gap_exp"), 1)
            flat = top_w[:].rearrange("p b s -> p (b s)")
            dve.tensor_reduce(flat, gap[:].rearrange("p b s e -> p (b s) e"), AX, ALU.add).then_inc(sem("top_w"), 1)
            dve.tensor_scalar(kept[:], slot_f[:], float(E * CP), None, ALU.is_lt).then_inc(sem("top_w"), 1)
            dve.wait_ge(sem("top_w"), 2)
            dve.reciprocal(top_w[:], top_w[:]).then_inc(sem("top_w"), 1)
            dve.wait_ge(sem("top_w"), 3)
            dve.tensor_tensor(top_w[:], top_w[:], kept[:], ALU.mult).then_inc(sem("top_w"), 1)
            dve.wait_ge(sem("top_w"), 4)

            def mixed(b):
                st = Steps(dve, sem("mixed"), "mixed", b)
                dve.wait_ge(sem(f"y_in{b % 2}"), 16 * SLOTS * (b // 2 + 1))
                if b >= 2:
                    dve.wait_ge(sem("roots4"), b - 1)
                y, mask = yg[b % 2], good[:].bitcast(I32)
                st(dve.tensor_tensor(y[:], y[:], bc(top_w[:, b, :], D), ALU.mult))
                st.sync()
                st(dve.tensor_scalar(zt[:], y[:], FMAX, None, ALU.is_gt))
                st(dve.tensor_scalar(mask, y[:], 0.0, 0.0, ALU.mult, ALU.is_equal))
                st.sync()
                st(dve.scalar_tensor_tensor(out=xt[:], in0=y[:], scalar=-FMAX, in1=zt[:], op0=ALU.is_lt, op1=ALU.subtract))
                st.sync()
                st(dve.tensor_scalar(xt[:], xt[:], -1.0e4, None, ALU.mult))
                st.sync()
                st(dve.copy_predicated(xt[:], mask, y[:]))
                st.sync()
                st(dve.tensor_tensor(H[:, b], H[:, b], xt[:], ALU.add))
                st.sync()
                norm_stats(dve, st, H[:, b], mv1[b % 2])
                st.close()

            def norm4(b):
                st = Steps(dve, sem("norm4"), "norm4", b)
                dve.wait_ge(sem("roots4"), b + 1)
                dve.wait_ge(sem("mixed"), (b + 1) * PER["mixed"])
                if b >= 2:
                    dve.wait_ge(sem("t4"), b - 1)
                st(dve.reciprocal(rs[:, 0, :], sd2[b % 2][:]))
                st(dve.tensor_tensor(zt[:], H[:, b], bc(mv1[b % 2][:, :, 0], D), ALU.subtract))
                st.sync()
                st(dve.tensor_tensor(X[:, b], zt[:], bc(rs[:, 0, :], D), ALU.mult))
                st.sync()
                high_low(dve, st, hl1[b % 2], X[:, b])
                st.close()
                st.sync()

            def kv_b(b):
                dve.wait_ge(sem("kv_prod"), b + 1)
                dve.tensor_tensor(kvt[:], wide(0), bs(w["kv_b"][:], SLOTS), ALU.add).then_inc(sem("kv_b"), 1)

            def sum_squares(b):
                dve.wait_ge(sem("ksq"), b + 1)
                if b >= 1:
                    dve.wait_ge(sem("roots_kv"), b)
                dve.tensor_reduce(ssq, groups(ksq[:]), AX, ALU.add).then_inc(sem("ssq"), 1)

            def kvnorm(b):
                st = Steps(dve, sem("kvnorm"), "kvnorm", b)
                dve.wait_ge(sem("roots_kv"), b + 1)
                if b >= 1:
                    dve.wait_ge(sem("gram"), b)
                st(dve.tensor_scalar(krs, ksd, EPS, None, ALU.add))
                st.sync()
                st(dve.reciprocal(krs, krs))
                st.sync()
                for side in range(2):
                    ins = dve.tensor_tensor(kvn[:, :, side, 0:D].rearrange("p s (g c) -> p s g c", c=HC), groups(kvt[:, :, side * D:(side + 1) * D]),
                                            krs[:, :, side * 16:(side + 1) * 16].unsqueeze(3).to_broadcast([P, SLOTS, 16, HC]), ALU.mult)
                st(ins)
                st.close()
                st.sync()

            def copy_out(name, product, dst, src):
                def f(b):
                    dve.wait_ge(sem(product), b + 1)
                    dve.tensor_copy(dst, src).then_inc(sem(name), 1)
                return f

            def own_heads(b):
                dve.wait_ge(sem("p2"), b + 1)
                dve.tensor_tensor(kv_s, bank(5)[0:D, 0:D], w["heads"][:], ALU.mult).then_inc(sem("kv_s"), 1)

            def add_input(b):
                dve.wait_ge(sem("p3"), b + 1)
                dve.tensor_tensor(a_s, bank(5)[0:D, 0:D + 1], w["eye"][:], ALU.add).then_inc(sem("a_s"), 1)

            def fold(b):
                st = Steps(dve, sem("fold"), "fold", b)
                dve.wait_ge(sem("p4"), b + 1)
                if b >= 1:
                    dve.wait_ge(sem("proj"), b)
                st(dve.tensor_copy(fold_w[0], bank(5)[:, 0:D]))
                st.sync()
                st(dve.tensor_tensor(fold_w[1], bank(5)[:, 0:D], fold_w[0].bitcast(F32), ALU.subtract))
                st(dve.tensor_tensor(fold_b, bank(5)[:, D:2 * D], w["bp"][:], ALU.add))
                st.close()
                st.sync()

            def pre_bias(b):
                dve.wait_ge(sem("proj"), b + 1)
                if b >= 1:
                    dve.wait_ge(sem("gelu_proj"), b)
                dve.tensor_tensor(pre[:], bank(1)[:, 0:SLOTS * D].rearrange("p (s c) -> p s c", s=SLOTS), bs(fold_b, SLOTS), ALU.add).then_inc(sem("pre"), 1)

            def resid2(b):
                st = Steps(dve, sem("resid2"), "resid2", b)
                dve.wait_ge(sem("gelu_proj"), b + 1)
                if b >= 2:
                    dve.wait_ge(sem("roots5"), b - 1)
                st(dve.tensor_tensor(H[:, b], H[:, b], gel[:], ALU.add))
                st.sync()
                st(dve.tensor_tensor(H[:, b], H[:, b], X[:, b], ALU.add))
                st.sync()
                norm_stats(dve, st, H[:, b], mv2[b % 2])
                st.close()

            def norm5(b):
                st = Steps(dve, sem("norm5"), "norm5", b)
                dve.wait_ge(sem("roots5"), b + 1)
                dve.wait_ge(sem("resid2"), (b + 1) * PER["resid2"])
                if b >= 2:
                    dve.wait_ge(sem("t5"), b - 1)
                st(dve.reciprocal(rs[:], sd1[b % 2][:]))
                st(dve.tensor_tensor(zt[:], H[:, b], bc(mv2[b % 2][:, :, 0], D), ALU.subtract))
                st.sync()
                st(dve.tensor_tensor(ratio[b % 2][:], sd1[b % 2][:, 1, :], rs[:, 0, :], ALU.mult))
                st(dve.tensor_tensor(xt[:], zt[:], bc(rs[:, 1, :], D), ALU.mult))
                st.sync()
                high_low(dve, st, hl3[b % 2], xt[:])
                st.close()
                st.sync()

            def first_of_largest(st, dst):
                st(dve.tensor_reduce(qq[:], eq[:], AX, ALU.max))
                st.sync()
                st(dve.tensor_tensor(dst, eq[:], bc(qq[:], E), ALU.is_equal))
                st.sync()

            def route_a(b):
                st = Steps(dve, sem("route_a"), "route_a", b)
                dve.wait_ge(sem("route_prod"), b + 1)
                if b >= 1:
                    dve.wait_ge(sem("share"), b)
                first = oh[0][:, 0:SLOTS, :]
                st(dve.tensor_tensor(lg[:], bank(1)[:, 0:SLOTS * E].rearrange("p (s e) -> p s e", s=SLOTS), bc(ratio[b % 2][:], E), ALU.mult))
                st.sync()
                st(dve.tensor_tensor(lg[:], lg[:], bs(w["br"][:], SLOTS), ALU.add))
                st.sync()
                st(dve.tensor_reduce(mx[:], lg[:], AX, ALU.max))
                st.sync()
                st(dve.tensor_tensor(lg[:], lg[:], bc(mx[:], E), ALU.subtract))
                st.sync()
                st(dve.scalar_tensor_tensor(out=eq[:], in0=lg[:], scalar=0.0, in1=w["order"][:], op0=ALU.is_ge, op1=ALU.mult))
                st.sync()
                first_of_largest(st, first)
                st(dve.scalar_tensor_tensor(out=lg[:], in0=first, scalar=-1.0e30, in1=lg[:], op0=ALU.mult, op1=ALU.add))
                st.sync()
                st(dve.tensor_reduce(mx[:], lg[:], AX, ALU.max))
                st.sync()
                st(dve.tensor_tensor(lg[:], lg[:], bc(mx[:], E), ALU.subtract))
                st.close()
                st.sync()

            def route_b(b):
                st = Steps(dve, sem("route_b"), "route_b", b)
                dve.wait_ge(sem("share"), b + 1)
                if b >= 2:
                    dve.wait_ge(sem("weigh"), 2 * POS * (b - 1))
                first = oh[0][:, 0:SLOTS, :]
                st(dve.scalar_tensor_tensor(out=eq[:], in0=lg[:], scalar=0.0, in1=w["order"][:], op0=ALU.is_ge, op1=ALU.mult))
                st.sync()
                first_of_largest(st, oh2[:])
                st(dve.tensor_scalar(qq[:], ex[:], 1.0, None, ALU.add))
                st.sync()
                st(dve.reciprocal(qq[:], qq[:]))
                st.sync()
                dve.tensor_tensor(oh2[:], oh2[:], bc(ex[:], E), ALU.mult).then_inc(sem("route_c"), 1)
                dve.wait_ge(sem("route_c"), 2 * b + 1)
                dve.tensor_tensor(oh2[:], oh2[:], first, ALU.add).then_inc(sem("route_c"), 1)
                dve.wait_ge(sem("route_c"), 2 * b + 2)
                st(dve.tensor_tensor(w8[b % 2][:], oh2[:], bc(qq[:], E), ALU.mult))
                st.close()
                st.sync()

            def weigh(n):
                b, side, p = unit(n)
                _, _, s0, s1 = PARTS[side]
                dve.wait_ge(sem("back"), n + 1)
                prod = bank(7)[:, 0:(s1 - s0) * P].rearrange("p (s e c) -> p s e c", s=s1 - s0, e=2)
                share = w8[b % 2][:, s0:s1, 2 * p:2 * p + 2].unsqueeze(3).to_broadcast([P, s1 - s0, 2, D])
                a = acc[:, s0:s1]
                if n:
                    dve.wait_ge(sem("weigh"), 2 * n)
                if p == 0:
                    dve.tensor_tensor(a, prod, share, ALU.mult).then_inc(sem("weigh"), 2)
                else:
                    t = tmp[n % 2][:, 0:s1 - s0]
                    dve.tensor_tensor(t, prod, share, ALU.mult).then_inc(sem("weigh"), 1)
                    dve.wait_ge(sem("weigh"), 2 * n + 1)
                    dve.tensor_tensor(a, a, t, ALU.add).then_inc(sem("weigh"), 1)
                if p == E // 2 - 1:
                    dve.wait_ge(sem("weigh"), 2 * n + 2)
                    h = H[:, b, s0:s1, :]
                    dve.tensor_tensor(h, h, a[:, :, 0, :], ALU.add).then_inc(sem("finish"), 1)
                    dve.wait_ge(sem("finish"), 4 * b + 2 * side + 1)
                    dve.tensor_tensor(h, h, a[:, :, 1, :], ALU.add).then_inc(sem("finish"), 1)
                    dve.wait_ge(sem("finish"), 4 * b + 2 * side + 2)

            table = dict(mixed=mixed, norm4=norm4, kv_b=kv_b, sum_squares=sum_squares, kvnorm=kvnorm, own_heads=own_heads, add_input=add_input, fold=fold,
                         pre_bias=pre_bias, resid2=resid2, norm5=norm5, route_a=route_a, route_b=route_b,
                         gram_s=copy_out("gram_s", "gram", gram_s, bank(5)[0:D + 1, 0:D + 1]),
                         p1_s=copy_out("p1_s", "p1", p1_s, bank(5)[0:D + 1, 0:D]))
            for step in range(STEPS2):
                for pos in range(POS):
                    n = (step - LAG2["moe"]) * POS + pos
                    for stage, when, f in DVE_ORDER:
                        if when == pos and at2(step, stage) is not None:
                            table[f](at2(step, stage))
                    if 0 <= n - 2 < NB * POS:
                        weigh(n - 2)

        PE_ORDER = (("norm5", 1, "t5"), ("fold", 2, "gram"), ("norm5", 2, "route"), ("kv", 3, "t4"), ("fold", 3, "gains_k"), ("fold", 4, "gains_v"),
                    ("fold", 5, "by_q"), ("kv", 5, "kv"), ("fold", 6, "by_proj"), ("fold", 7, "proj"))
        ACT_ORDER = (("kv", 0, "roots4"), ("fold", 0, "roots_kv"), ("norm5", 0, "roots5"), ("norm5", 1, "stack5"), ("kv", 3, "stack4"),
                     ("kv", 6, "square"), ("fold", 7, "gelu_proj"))
        DVE_ORDER = (("norm5", 0, "norm5"), ("fold", 1, "kvnorm"), ("fold", 2, "gram_s"), ("kv", 2, "norm4"), ("norm5", 3, "route_a"), ("fold", 3, "p1_s"),
                     ("fold", 4, "own_heads"), ("mixed", 4, "mixed"), ("fold", 5, "add_input"), ("kv", 5, "kv_b"), ("norm5", 5, "route_b"), ("fold", 6, "fold"),
                     ("kv", 6, "sum_squares"), ("fold", 7, "pre_bias"), ("fold", 7, "resid2"))

        def store_expert(sp, e):
            sp.wait_ge(sem("b_yo"), UE * (e + 1))
            sp.dma_start(expert_out[e * CP:(e + 1) * CP, :].rearrange("(p t) c -> p t c", p=P), yo[e % 2][:]).then_inc(sem(f"expert_out{e % 2}"), 16)

        @block.sync
        def _(sp):
            sp.dma_start(patches, i["patches"]).then_inc(sem("patches_in"), 16)
            for n in loads:
                sp.dma_start(w[n][:], i[n]).then_inc(sem("weights_in"), 16)
            sp.dma_start(ew1, i["ew1"]).then_inc(sem("weights_in"), 16)
            sp.dma_start(fw1, i["fw1"]).then_inc(sem("weights_in"), 16)
            sp.wait_ge(sem("zero_set"), 1)
            for e in range(E):
                sp.dma_start(slots_buf[e * CP:(e + 1) * CP, :].rearrange("(p t) c -> p t c", p=P), zeros[:].unsqueeze(1).to_broadcast([P, ET, 2 * D])).then_inc(sem("slots_zeroed"), 16)
            for k in range(4):
                sp.wait_ge(sem(f"scattered{k}"), 16 * SLOTS * NB // 4)
            for e in range(E):
                if e >= 2:
                    sp.wait_ge(sem("b_turn"), UE * (e - 1))
                sp.dma_start(xl[e % 2][:], slots_buf[e * CP:(e + 1) * CP, :].rearrange("(p t) c -> p t c", p=P)).then_inc(sem(f"xl_in{e % 2}"), 16)
                if e >= 1:
                    store_expert(sp, e - 1)
            store_expert(sp, E - 1)
            outputs(sp)

        @block.gpsimd
        def _(pool):
            pool.dma_start(w["ids"][:], i["ids"]).then_inc(sem("ids_in"), 16)
            pool.wait_ge(sem("ids_in"), 16)

            def gather(b):
                if b >= 2:
                    pool.wait_ge(sem("norm1a"), (b - 2) * PER["norm1a"] + 1)
                for t in range(TXT):
                    pool.indirect_dma_start(emb[b % 2][:, t, :], None, i["table"], bass.IndirectOffsetOnAxis(w["ids"][:, b * TXT + t:b * TXT + t + 1], 0)).then_inc(sem(f"gathered{b % 2}"), 16)

            def scatter(b):
                if b == 0:
                    pool.wait_ge(sem("slots_zeroed"), 16 * E)
                pool.wait_ge(sem("place"), (b + 1) * PER["place"])
                for s in range(SLOTS):
                    rows = P if s < TXT else N_IMG
                    pool.indirect_dma_start(slots_buf, bass.IndirectOffsetOnAxis(slot_i[0:rows, b, s:s + 1], 0), hl3[b % 4][0:rows, s, :], None,
                                            bounds_check=E * CP - 1, oob_is_err=False).then_inc(sem(f"scattered{b % 4}"), 16)

            for step in range(STEPS):
                for stage, f in (("gather", gather), ("scatter", scatter)):
                    if (b := at(step, stage)) is not None:
                        f(b)
            pool_second(pool)

        banks = Banks()

        def turn(pe, src, dst_bank, cols=(2 * D)):
            for s in range(SLOTS):
                rows = P if s < TXT else N_IMG
                last = pe.transpose(bank(dst_bank, 2)[0:cols, s * P:s * P + rows], src[0:rows, s, :], ident[0:rows, 0:rows])
            return last

        def turn_back(pe, src, k):
            pe.transpose(bank(k)[:, 0:P], src[:, 0:P], ident[:])
            pe.transpose(bank(k)[:, P:2 * P], src[:, P:2 * P], ident[:])
            return pe.transpose(bank(k)[0:N_IMG, 2 * P:2 * P + D], src[D:P, LEFT:RIGHT], ident[D:P, D:P])

        def two(pe, dst, parts, rhs, cols=slice(None)):
            pe.matmul(dst, parts[0][:, cols], rhs, start=True, stop=False)
            return pe.matmul(dst, parts[1][:, cols], rhs, start=False, stop=True)

        def tokens_by(pe, dst, stack, parts, cols):
            for s in range(SLOTS):
                pe.matmul(dst[:, s, :], stack[:, s * P:(s + 1) * P], parts[0][:, cols], start=True, stop=False)
                last = pe.matmul(dst[:, s, :], stack[:, s * P:(s + 1) * P], parts[1][:, cols], start=False, stop=True)
            return last

        @block.tensor
        def _(pe):
            pe.wait_ge(sem("weights_in"), LOADED)
            pe.wait_ge(sem("zero_set"), 1)
            pe.matmul(bank(7)[:, 0:1], w["wq"][0:D, :], w["norm_b"][:], start=True, stop=True)
            pe.matmul(bank(7)[:, 1:2], w["wk"][0:D, :], w["norm_b"][:], start=True, stop=True)
            pe.matmul(bank(7)[:, 64:64 + D], w["norm_b"][:].to_broadcast([D, P]), w["wv"][0:D, :], start=True, stop=True)
            for k in range(E * J):
                last = pe.matmul(bank(7)[:, 8 + k:9 + k], fw1[0:D, k * P:(k + 1) * P], w["fln_b"][:, k // J:k // J + 1], start=True, stop=True)
            last.then_inc(sem("bias_prod"), 1)
            pe.wait_ge(sem("patches_in"), 16)
            for h in range(2):
                for k in range(KC):
                    last = pe.matmul(bank(h)[0:D, 0:NB * N_IMG // 2], w["tok_w"][:, k, :], patches[:, k, h * NB * N_IMG // 2:(h + 1) * NB * N_IMG // 2],
                                     start=(k == 0), stop=(k == KC - 1))
            last.then_inc(sem("patch_prod"), 1)
            pe.wait_ge(sem("img_t"), 2)
            for b in range(NB):
                last = pe.transpose(bank(2 + b // 8)[0:N_IMG, (b % 8) * D:(b % 8 + 1) * D], img_t[:, b * N_IMG:(b + 1) * N_IMG], ident[0:D, 0:D])
            last.then_inc(sem("img_turn"), 1)
            pe.wait_ge(sem("prep"), 1)

            def t1(b):
                banks.take(pe, TURN, sem("xs1"), b + 1)
                pe.wait_ge(sem("norm1b"), (b + 1) * PER["norm1b"])
                turn(pe, hl1[b % 2], 0).then_inc(sem("t1"), 1)

            def q_or_k(b, name):
                banks.take(pe, WIDE, sem("qk_low"), b * PER["qk_low"] + (1 if name == "wq" else 3))
                pe.wait_ge(sem("xs1"), b + 1)
                for h in range(2):
                    last = two(pe, bank(2 + h)[:, 0:HALF], split[name], xs1[b % 2][:, h * HALF:(h + 1) * HALF])
                last.then_inc(sem("qk_prod"), 1)

            def q(b):
                q_or_k(b, "wq")

            def k(b):
                q_or_k(b, "wk")

            def v(b):
                banks.take(pe, LOW, sem("vals"), b + 1)
                pe.wait_ge(sem("xs1"), b + 1)
                tokens_by(pe, bank(7)[:, 0:SLOTS * D].rearrange("p (s c) -> p s c", s=SLOTS), xs1[b % 2], split["wv"], slice(0, D)).then_inc(sem("v_prod"), 1)

            spans = ((0, LEFT), (LEFT, N))

            def scores(b, s):
                if s == 0:
                    pe.wait_ge(sem("qk_low"), (b + 1) * PER["qk_low"])
                for h, (a, z) in enumerate(spans):
                    n = b * 2 * SLOTS + 2 * s + h
                    banks.take(pe, (SCORE[h],), sem("relu"), n + 1)
                    dst = bank(SCORE[h])[:, 0:z - a]
                    pe.matmul(dst, kh[b % 2][:, s * P:(s + 1) * P], qst[b % 2][:, a:z], start=True, stop=False)
                    pe.matmul(dst, kl[b % 2][:, s * P:(s + 1) * P], qst[b % 2][:, a:z], start=False, stop=True).then_inc(sem("scores"), 1)

            def attend(b, s):
                if s == 0:
                    banks.take(pe, MIX, sem("ot"), b + 1)
                    pe.wait_ge(sem("vals"), (b + 1) * PER["vals"])
                pe.wait_ge(sem("relu"), b * 2 * SLOTS + 2 * s + 2)
                for h, (a, z) in enumerate(spans):
                    last = pe.matmul(bank(6)[h * D:(h + 1) * D, 0:z - a], vv[b % 2][:, s, :], prob[s][:, a:z], start=(s == 0), stop=(s == SLOTS - 1))
                last.then_inc(sem("attend"), 1)

            def o_turn(b):
                banks.take(pe, TURN, sem("resid"), b * PER["resid"] + 2)
                pe.wait_ge(sem("ot"), b + 1)
                turn_back(pe, ot[b % 2], 0).then_inc(sem("o_turn"), 1)

            def t2(b):
                banks.take(pe, TURN, sem("xs2"), b + 1)
                pe.wait_ge(sem("resid"), (b + 1) * PER["resid"])
                turn(pe, hl2[b % 2], 0).then_inc(sem("t2"), 1)

            def ffn1(b):
                banks.take(pe, WIDE, sem("ff"), b + 1)
                pe.wait_ge(sem("xs2"), b + 1)
                for h in range(2):
                    last = two(pe, bank(2 + h)[:, 0:HALF], split["w1"], xs2[b % 2][:, h * HALF:(h + 1) * HALF])
                last.then_inc(sem("ffn1"), 1)

            def ffn2(b):
                banks.take(pe, LOW, sem("yt"), b + 1)
                pe.wait_ge(sem("ff"), b + 1)
                for h, (a, z) in enumerate(spans):
                    last = pe.matmul(bank(7)[h * D:(h + 1) * D, 0:z - a], w["w2"][:], ff[b % 2][:, a:z], start=True, stop=True)
                last.then_inc(sem("ffn2"), 1)

            def y_turn(b):
                banks.take(pe, TURN, sem("norm2a"), b * PER["norm2a"] + 2)
                pe.wait_ge(sem("yt"), b + 1)
                turn_back(pe, yt[b % 2], 0).then_inc(sem("y_turn"), 1)

            def t3(b):
                banks.take(pe, TURN, sem("xs3"), b + 1)
                pe.wait_ge(sem("norm3b"), (b + 1) * PER["norm3b"])
                turn(pe, hl3[b % 4], 0).then_inc(sem("t3"), 1)

            def gate(b):
                banks.take(pe, LOW, sem("gate"), b * PER["gate"] + 1)
                pe.wait_ge(sem("xs3"), b + 1)
                tokens_by(pe, bank(7)[:, 0:SLOTS * E].rearrange("p (s e) -> p s e", s=SLOTS), xs3[b % 2], split["gw"], slice(0, E)).then_inc(sem("gate_prod"), 1)

            def count(b):
                banks.take(pe, LOW, sem("place"), b * PER["place"] + 2)
                pe.wait_ge(sem("gate"), (b + 1) * PER["gate"])
                o, dst = oh_b[b % 2], bank(7)[:, 0:(SLOTS + 1) * E].rearrange("p (s e) -> p s e", e=E)
                last = pe.matmul(dst, tri_b[:], o[:], start=True, stop=False, skip_group_check=True)
                for s in (IMG, 0, 1, 2, 3):
                    rows = N_IMG if s == IMG else P
                    first = 0 if s == IMG else s + 1
                    if first < TXT:
                        pe.matmul(dst[:, first:TXT, :], ones_b[0:rows, :], bs(o[0:rows, s, :], TXT - first), start=False, stop=False, skip_group_check=True)
                    last = pe.matmul(dst[:, SLOTS, :], ones_b[0:rows, :], o[0:rows, s, :], start=False, stop=(s == 3), skip_group_check=True)
                last.then_inc(sem("count"), 1)

            for step in range(STEPS):
                A, Q, R, Y, G = (at(step, k) for k in ("attn", "qkv", "resid", "ffn2", "gate"))
                for s in range(SLOTS + 1):
                    if A is not None and s < SLOTS:
                        scores(A, s)
                    for stage, when, f in ((G, 0, t3), (Y, 0, ffn2), (Q, 1, t1), (G, 1, gate), (R, 2, o_turn), (Q, 2, q),
                                           (Q, 3, v), (Y, 3, y_turn), (Q, 4, k), (R, 4, t2), (G, 5, count), (R, 5, ffn1)):
                        if when == s and stage is not None:
                            f(stage)
                    if A is not None and s >= 1:
                        attend(A, s - 1)

            def b_turn(u):
                e, c = B_STEPS[u]
                if c == 0:
                    pe.wait_ge(sem(f"xl_in{e % 2}"), 16 * (e // 2 + 1))
                banks.take(pe, (u % 2,), sem("b_bx"), u + 1)
                for k, t in enumerate(range(c, min(c + 4, ET))):
                    last = pe.transpose(bank(u % 2)[:, k * P:(k + 1) * P], xl[e % 2][:, t, :], ident[:])
                last.then_inc(sem("b_turn"), 1)

            def b_up(u):
                e, c = B_STEPS[u]
                n = P * (min(c + 4, ET) - c)
                pe.wait_ge(sem("b_bx"), u + 1)
                for j in range(J):
                    banks.take(pe, (2 + j,), sem(f"b_relu{j}"), u + 1)
                    two(pe, bank(2 + j)[:, 0:n], split["ew1"], bx[u % 2][:, 0:n], slice((e * J + j) * P, (e * J + j + 1) * P)).then_inc(sem(f"b_up{j}"), 1)

            def b_down(u):
                e, c = B_STEPS[u]
                n = P * (min(c + 4, ET) - c)
                banks.take(pe, (4 + u % 2,), sem("b_by"), u + 1)
                for j in range(J):
                    pe.wait_ge(sem(f"b_relu{j}"), u + 1)
                    for h, (a, z) in enumerate(((0, LEFT), (LEFT, n))):
                        last = pe.matmul(bank(4 + u % 2)[h * D:(h + 1) * D, 0:z - a], w["ew2"][:, e * J + j, :], bg[u % 2][:, j, a:z], start=(j == 0), stop=(j == J - 1))
                last.then_inc(sem("b_down"), 1)

            def b_back(u):
                e, c = B_STEPS[u]
                banks.take(pe, (6 + u % 2,), sem("b_yo"), u + 1)
                pe.wait_ge(sem("b_by"), u + 1)
                pe.transpose(bank(6 + u % 2)[:, 0:P], by[u % 2][:, 0:P], ident[:])
                rows = P if c + 4 <= ET else D
                pe.transpose(bank(6 + u % 2)[:, P:P + rows], by[u % 2][0:rows, P:2 * P], ident[0:rows, 0:rows]).then_inc(sem("b_back"), 1)

            for step in range(NU + 3):
                for lag, f in ((0, b_turn), (1, b_up), (2, b_down), (3, b_back)):
                    if 0 <= step - lag < NU:
                        f(step - lag)
            pe_second(pe)

        @block.scalar
        def _(act):
            act.wait_ge(sem("weights_in"), LOADED)
            act.wait_ge(sem("zero_set"), 1)
            act.wait_ge(sem("patch_prod"), 1)
            for h in range(2):
                act.activation(img_t[:, h * NB * N_IMG // 2:(h + 1) * NB * N_IMG // 2], bank(h)[0:D, 0:NB * N_IMG // 2], ACT.Identity, bias=w["tok_b"][:]).then_inc(sem("img_t"), 1)
            act.wait_ge(sem("img_turn"), 1)
            act.activation(H[0:N_IMG, :, IMG, :], bank(2, 2)[0:N_IMG, :].rearrange("p (b c) -> p b c", b=NB), ACT.Identity).then_inc(sem("img_h"), 1)
            act.wait_ge(sem("prep"), 1)

            def roots1(b):
                act.wait_ge(sem("norm1a"), (b + 1) * PER["norm1a"])
                if b >= 2:
                    act.wait_ge(sem("norm1b"), (b - 2) * PER["norm1b"] + 1)
                act.activation(sd1[b % 2][:, 0, :], mv1[b % 2][:, :, 1], ACT.Sqrt, bias=eps_t[:, 0:1])
                act.activation(sd1[b % 2][:, 1, :], mv1[b % 2][:, :, 1], ACT.Sqrt, bias=eps_t[:, 1:2], scale=1.0 + EPS).then_inc(sem("roots1"), 1)

            def stack1(b):
                act.wait_ge(sem("t1"), b + 1)
                if b >= 2:
                    act.wait_ge(sem("v_prod"), b - 1)
                    act.wait_ge(sem("qk_prod"), 2 * (b - 1))
                act.activation(xs1[b % 2][:, 0:N], bank(0, 2)[:, 0:N], ACT.Identity).then_inc(sem("xs1"), 1)

            def q_high(b):
                act.wait_ge(sem("qk_prod"), 2 * b + 1)
                if b >= 2:
                    act.wait_ge(sem("scores"), (b - 1) * 2 * SLOTS)
                act.activation(qst[b % 2][:].rearrange("p (h n) -> p h n", h=2), halves(2), ACT.Identity, bias=bq[:]).then_inc(sem("qk_high"), 1)

            def k_high(b):
                act.wait_ge(sem("qk_prod"), 2 * b + 2)
                act.activation(kh[b % 2][:, 0:N].rearrange("p (h n) -> p h n", h=2), halves(2), ACT.Identity, bias=bk[:]).then_inc(sem("qk_high"), 1)

            def relu(b, s):
                for h, (a, z) in enumerate(((0, LEFT), (LEFT, N))):
                    act.wait_ge(sem("scores"), b * 2 * SLOTS + 2 * s + h + 1)
                    if b >= 1 and h == 0:
                        act.wait_ge(sem("attend"), (b - 1) * SLOTS + s + 1)
                    act.activation(prob[s][:, a:z], bank(SCORE[h])[:, 0:z - a], ACT.Relu, scale=SCALE).then_inc(sem("relu"), 1)

            def o_copy(b):
                act.wait_ge(sem("attend"), (b + 1) * SLOTS)
                if b >= 2:
                    act.wait_ge(sem("o_turn"), b - 1)
                act.activation(ot[b % 2][:], bank(6)[:, 0:RIGHT], ACT.Identity).then_inc(sem("ot"), 1)

            def stack2(b):
                act.wait_ge(sem("t2"), b + 1)
                if b >= 2:
                    act.wait_ge(sem("ffn1"), b - 1)
                act.activation(xs2[b % 2][:, 0:N], bank(0, 2)[:, 0:N], ACT.Identity).then_inc(sem("xs2"), 1)

            def ffn_relu(b):
                act.wait_ge(sem("ffn1"), b + 1)
                if b >= 2:
                    act.wait_ge(sem("ffn2"), b - 1)
                act.activation(ff[b % 2][:].rearrange("p (h n) -> p h n", h=2), halves(2), ACT.Relu, bias=w["b1"][:]).then_inc(sem("ff"), 1)

            def y_copy(b):
                act.wait_ge(sem("ffn2"), b + 1)
                if b >= 2:
                    act.wait_ge(sem("y_turn"), b - 1)
                act.activation(yt[b % 2][:], bank(7)[:, 0:RIGHT], ACT.Identity, bias=w["b2"][:]).then_inc(sem("yt"), 1)

            def root(b, which, mv, sd):
                act.wait_ge(sem(which + "a"), (b + 1) * PER[which + "a"])
                if b >= 2:
                    act.wait_ge(sem(which + "b"), (b - 2) * PER[which + "b"] + 1)
                act.activation(sd[b % 2][:], mv[b % 2][:, :, 1], ACT.Sqrt, bias=eps_t[:, 0:1]).then_inc(sem("root_" + which), 1)

            def root2(b):
                root(b, "norm2", mv2, sd2)

            def root3(b):
                root(b, "norm3", mv3, sd3)

            def stack3(b):
                act.wait_ge(sem("t3"), b + 1)
                if b >= 2:
                    act.wait_ge(sem("gate_prod"), b - 1)
                act.activation(xs3[b % 2][:, 0:N], bank(0, 2)[:, 0:N], ACT.Identity).then_inc(sem("xs3"), 1)

            for step in range(STEPS):
                A, Q, R, Y, G, N1 = (at(step, k) for k in ("attn", "qkv", "resid", "ffn2", "gate", "norm1"))
                for s in range(SLOTS + 1):
                    if A is not None and s < SLOTS:
                        relu(A, s)
                    for stage, when, f in ((Y, 0, y_copy), (G, 0, stack3), (Q, 1, stack1), (Q, 2, q_high), (N1, 2, roots1),
                                           (Q, 4, k_high), (Y, 4, root2), (R, 4, stack2), (R, 5, ffn_relu), (A, 5, o_copy), (Y, 5, root3)):
                        if when == s and stage is not None:
                            f(stage)

            act.wait_ge(sem("place"), NB * PER["place"])
            act.activation(gap[:], gap[:], ACT.Exp).then_inc(sem("gap_exp"), 1)

            def b_stack(u):
                e, c = B_STEPS[u]
                n = P * (min(c + 4, ET) - c)
                act.wait_ge(sem("b_turn"), u + 1)
                if u >= 2:
                    act.wait_ge(sem("b_up1"), u - 1)
                act.activation(bx[u % 2][:, 0:n], bank(u % 2)[:, 0:n], ACT.Identity).then_inc(sem("b_bx"), 1)

            def b_relu0(u):
                e, c = B_STEPS[u]
                n = P * (min(c + 4, ET) - c)
                act.wait_ge(sem("b_up0"), u + 1)
                if u >= 2:
                    act.wait_ge(sem("b_down"), u - 1)
                act.activation(bg[u % 2][:, 0, 0:n], bank(2)[:, 0:n], ACT.Relu, bias=w["eb1"][:, e * J:e * J + 1]).then_inc(sem("b_relu0"), 1)

            for step in range(NU + 1):
                for lag, f in ((0, b_stack), (1, b_relu0)):
                    if 0 <= step - lag < NU:
                        f(step - lag)
            act_second(act)

        def norm_stats(dve, st, src, mv):
            for s in range(SLOTS):
                st(dve.bn_stats(stats[:, s, :], src[:, s, :]))
            st.sync()
            for s in range(SLOTS):
                st(dve.bn_aggr(mv[:, s, :], stats[:, s, :]))

        def high_low(dve, st, dst, src):
            st(dve.tensor_copy(dst[:, :, 0:D].bitcast(F32R), src))
            st.sync()
            st(dve.tensor_tensor(dst[:, :, D:2 * D].bitcast(F32R), src, dst[:, :, 0:D], ALU.subtract))

        @block.vector
        def _(dve):
            n_prep = [0]

            def step_of(ins):
                ins.then_inc(sem("prep_steps"), 1)
                n_prep[0] += 1

            def sync():
                dve.wait_ge(sem("prep_steps"), n_prep[0])

            step_of(dve.memset(zeros[:], 0.0))
            for tile in (H, psum, *hl1, *hl2, *hl3, *rr, *oh, *uu):
                step_of(dve.memset(tile[:], 0.0))
            for tile in (*xs1, *xs2, *xs3, *kh, *kl):
                step_of(dve.memset(tile[:, N:NPAD].bitcast(F32), 0.0))
            step_of(dve.memset(eps_t[:, 0:1], EPS))
            step_of(dve.memset(eps_t[:, 1:2], EPS * EPS))
            step_of(dve.memset(ones_b[:], 1.0))
            sync()
            dve.engine_nop().then_inc(sem("zero_set"), 1)
            dve.wait_ge(sem("weights_in"), LOADED)
            step_of(dve.tensor_copy(tri_b[:], w["tri"][:]))
            step_of(dve.tensor_copy(carry[:], w["base"][:]))
            g1 = w["norm_g"][:, 0:1]
            kv = w["wkv"][:].rearrange("p (g c) -> p g c", c=HC)
            kb = w["kv_b"][:].rearrange("p (g c) -> p g c", c=HC)
            step_of(dve.tensor_reduce(ctr_w[:], kv, AX, ALU.add))
            step_of(dve.tensor_reduce(ctr_b[:], kb, AX, ALU.add))
            dve.wait_ge(sem("bias_prod"), 1)
            step_of(dve.tensor_tensor(bq[:], bank(7)[:, 0:1], w["bq"][:], ALU.add))
            step_of(dve.tensor_tensor(bk[:], bank(7)[:, 1:2], w["bk"][:], ALU.add))
            step_of(dve.tensor_tensor(bv[:], bank(7)[:, 64:64 + D], w["bv"][:], ALU.add))
            step_of(dve.tensor_tensor(fb1[:], bank(7)[:, 8:8 + E * J], w["fb1"][:], ALU.add))
            sync()
            step_of(dve.tensor_scalar(ctr_w[:], ctr_w[:], 1.0 / HC, None, ALU.mult))
            step_of(dve.tensor_scalar(ctr_b[:], ctr_b[:], 1.0 / HC, None, ALU.mult))
            for n in ("wq", "wk", "wv"):
                step_of(dve.tensor_scalar(w[n][:], w[n][:], g1, None, ALU.mult))
            for e in range(E):
                part = fw1[:, e * F_MOE:(e + 1) * F_MOE]
                step_of(dve.tensor_scalar(part, part, w["fln_g"][:, e:e + 1], None, ALU.mult))
            step_of(dve.tensor_tensor(ak[:], w["ak"][:], w["diag"][:], ALU.mult))
            step_of(dve.tensor_tensor(av[:], w["av"][:], w["diag"][:], ALU.mult))
            sync()
            step_of(dve.tensor_tensor(kv, kv, bc(ctr_w[:], HC), ALU.subtract))
            step_of(dve.tensor_tensor(kb, kb, bc(ctr_b[:], HC), ALU.subtract))
            sync()
            source = {"ew1": ew1, "fw1": fw1}
            for n, (hi, lo) in split.items():
                src = source[n] if n in source else w[n][:]
                step_of(dve.tensor_copy(hi[:], src))
            sync()
            for n, (hi, lo) in split.items():
                src = source[n] if n in source else w[n][:]
                step_of(dve.tensor_tensor(lo[:], src, hi[:].bitcast(F32), ALU.subtract))
            sync()
            dve.wait_ge(sem("img_h"), 1)
            dve.engine_nop().then_inc(sem("prep"), 1)

            def norm1a(b):
                st = Steps(dve, sem("norm1a"), "norm1a", b)
                dve.wait_ge(sem(f"gathered{b % 2}"), 16 * TXT * (b // 2 + 1))
                if b >= 2:
                    dve.wait_ge(sem("roots1"), b - 1)
                st(dve.tensor_tensor(H[:, b, 0:TXT, :], emb[b % 2][:], w["pe"][:], ALU.add))
                st.sync()
                norm_stats(dve, st, H[:, b], mv1[b % 2])
                st.close()

            def norm1b(b):
                st = Steps(dve, sem("norm1b"), "norm1b", b)
                dve.wait_ge(sem("roots1"), b + 1)
                dve.wait_ge(sem("norm1a"), (b + 1) * PER["norm1a"])
                if b >= 2:
                    dve.wait_ge(sem("t1"), b - 1)
                st(dve.reciprocal(rs[:], sd1[b % 2][:]))
                st(dve.tensor_tensor(zt[:], H[:, b], bc(mv1[b % 2][:, :, 0], D), ALU.subtract))
                st.sync()
                st(dve.tensor_tensor(xt[:], zt[:], bc(rs[:, 1, :], D), ALU.mult))
                st(dve.tensor_tensor(X[:, b], zt[:], bc(rs[:, 0, :], D), ALU.mult))
                st.sync()
                high_low(dve, st, hl1[b % 2], xt[:])
                st.close()
                st.sync()

            def q_low(b):
                dve.wait_ge(sem("qk_high"), 2 * b + 1)
                lo = qst[b % 2][D:P, :].rearrange("p (h n) -> p h n", h=2)
                dve.scalar_tensor_tensor(out=lo, in0=halves(2)[D:P], scalar=bq[D:P, 0:1], in1=lo.bitcast(F32), op0=ALU.add, op1=ALU.subtract).then_inc(sem("qk_low"), 1)

            def k_low(b):
                dve.wait_ge(sem("qk_high"), 2 * b + 2)
                hi = kh[b % 2][:, 0:N].rearrange("p (h n) -> p h n", h=2)
                lo = kl[b % 2][:, 0:N].rearrange("p (h n) -> p h n", h=2)
                dve.scalar_tensor_tensor(out=lo, in0=halves(2), scalar=bk[:, 0:1], in1=hi.bitcast(F32), op0=ALU.add, op1=ALU.subtract).then_inc(sem("qk_low"), 2)

            def vals(b):
                dve.wait_ge(sem("v_prod"), b + 1)
                if b >= 2:
                    dve.wait_ge(sem("attend"), (b - 1) * SLOTS)
                dve.tensor_tensor(vv[b % 2][:], bank(7)[:, 0:SLOTS * D].rearrange("p (s c) -> p s c", s=SLOTS), bs(bv[:], SLOTS), ALU.add).then_inc(sem("vals"), 1)

            def resid(b):
                st = Steps(dve, sem("resid"), "resid", b)
                dve.wait_ge(sem("o_turn"), b + 1)
                if b >= 2:
                    dve.wait_ge(sem("t2"), b - 1)
                r = rr[b % 2]
                st(dve.tensor_tensor(by_pairs(r), turned(0), by_pairs(X[:, b]), ALU.add))
                st(dve.tensor_tensor(r[0:N_IMG, IMG, :], bank(0)[0:N_IMG, 2 * P:2 * P + D], X[0:N_IMG, b, IMG, :], ALU.add))
                st.sync()
                high_low(dve, st, hl2[b % 2], r[:])
                st.close()

            def norm2a(b):
                st = Steps(dve, sem("norm2a"), "norm2a", b)
                dve.wait_ge(sem("y_turn"), b + 1)
                if b >= 2:
                    dve.wait_ge(sem("root_norm2"), b - 1)
                r, u = rr[b % 2], uu[b % 2]
                st(dve.tensor_tensor(by_pairs(u), turned(0), by_pairs(r), ALU.add))
                st(dve.tensor_tensor(u[0:N_IMG, IMG, :], bank(0)[0:N_IMG, 2 * P:2 * P + D], r[0:N_IMG, IMG, :], ALU.add))
                st.sync()
                norm_stats(dve, st, u[:], mv2[b % 2])
                st.close()

            def norm2b(b):
                st = Steps(dve, sem("norm2b"), "norm2b", b)
                dve.wait_ge(sem("root_norm2"), b + 1)
                dve.wait_ge(sem("norm2a"), (b + 1) * PER["norm2a"])
                st(dve.reciprocal(rs[:, 0, :], sd2[b % 2][:]))
                st(dve.tensor_tensor(zt[:], uu[b % 2][:], bc(mv2[b % 2][:, :, 0], D), ALU.subtract))
                st.sync()
                st(dve.tensor_tensor(zt[:], zt[:], bc(rs[:, 0, :], D), ALU.mult))
                st.sync()
                st(dve.tensor_tensor(zt[:], zt[:], bs(w["fg"][:], SLOTS), ALU.mult))
                st(dve.tensor_tensor(H[:, b], H[:, b], bs(w["fb"][:], SLOTS), ALU.add))
                st.sync()
                st(dve.tensor_tensor(H[:, b], H[:, b], zt[:], ALU.add))
                st.close()
                st.sync()

            def norm3a(b):
                st = Steps(dve, sem("norm3a"), "norm3a", b)
                if b >= 2:
                    dve.wait_ge(sem("root_norm3"), b - 1)
                norm_stats(dve, st, H[:, b], mv3[b % 2])
                st.close()

            def norm3b(b):
                st = Steps(dve, sem("norm3b"), "norm3b", b)
                dve.wait_ge(sem("root_norm3"), b + 1)
                dve.wait_ge(sem("norm3a"), (b + 1) * PER["norm3a"])
                if b >= 4:
                    dve.wait_ge(sem(f"scattered{b % 4}"), 16 * SLOTS * (b // 4))
                    dve.wait_ge(sem("t3"), b - 3)
                st(dve.reciprocal(rs[:, 0, :], sd3[b % 2][:]))
                st(dve.tensor_tensor(zt[:], H[:, b], bc(mv3[b % 2][:, :, 0], D), ALU.subtract))
                st.sync()
                st(dve.tensor_tensor(xt[:], zt[:], bc(rs[:, 0, :], D), ALU.mult))
                st.sync()
                high_low(dve, st, hl3[b % 4], xt[:])
                st.close()
                st.sync()

            def gate(b):
                st = Steps(dve, sem("gate"), "gate", b)
                dve.wait_ge(sem("gate_prod"), b + 1)
                if b >= 2:
                    dve.wait_ge(sem("count"), b - 1)
                st(dve.tensor_tensor(lg[:], bank(7)[:, 0:SLOTS * E].rearrange("p (s e) -> p s e", s=SLOTS), bs(w["gb"][:], SLOTS), ALU.add))
                st.sync()
                st(dve.tensor_reduce(mx[:], lg[:], AX, ALU.max))
                st.sync()
                st(dve.tensor_tensor(gap[:, b], lg[:], bc(mx[:], E), ALU.subtract))
                st.sync()
                st(dve.scalar_tensor_tensor(out=eq[:], in0=gap[:, b], scalar=0.0, in1=w["order"][:], op0=ALU.is_ge, op1=ALU.mult))
                st.sync()
                st(dve.tensor_reduce(mx[:], eq[:], AX, ALU.max))
                st.sync()
                st(dve.tensor_tensor(oh[b % 2][:, 0:SLOTS, :], eq[:], bc(mx[:], E), ALU.is_equal))
                st.sync()
                st(dve.tensor_copy(oh_b[b % 2][:], oh[b % 2][:]))
                st.close()

            def place(b):
                st = Steps(dve, sem("place"), "place", b)
                dve.wait_ge(sem("count"), b + 1)
                c = bank(7)[:, 0:(SLOTS + 1) * E].rearrange("p (s e) -> p s e", e=E)
                st(dve.tensor_tensor(pl[:], c[:, 0:SLOTS, :], bs(carry[:], SLOTS), ALU.add))
                st.sync()
                st(dve.tensor_tensor(carry[:], c[:, SLOTS, :], carry[:], ALU.add))
                st(dve.tensor_tensor(ov[:], pl[:], bs(w["limit"][:], SLOTS), ALU.is_ge))
                st.sync()
                st(dve.scalar_tensor_tensor(out=pl[:], in0=ov[:], scalar=DROPPED, in1=pl[:], op0=ALU.mult, op1=ALU.add))
                st.sync()
                st(dve.tensor_tensor(pl[:], pl[:], oh[b % 2][:, 0:SLOTS, :], ALU.mult))
                st.sync()
                st(dve.tensor_reduce(slot_f[:, b, :], pl[:], AX, ALU.add))
                st.sync()
                st(dve.tensor_copy(slot_i[:, b, :], slot_f[:, b, :]))
                st.close()
                st.sync()

            for step in range(STEPS):
                N1, A, Q, R, Y, G = (at(step, k) for k in ("norm1", "attn", "qkv", "resid", "ffn2", "gate"))
                for stage, f in ((G, gate), (N1, norm1a), (R, resid), (Q, q_low), (Q, vals), (Y, norm2a), (Q, k_low), (Y, norm2b),
                                 (Y, norm3a), (N1, norm1b), (Y, norm3b), (G, place)):
                    if stage is not None:
                        f(stage)

            def b_relu1(u):
                e, c = B_STEPS[u]
                n = P * (min(c + 4, ET) - c)
                dve.wait_ge(sem("b_up1"), u + 1)
                if u >= 2:
                    dve.wait_ge(sem("b_down"), u - 1)
                dve.tensor_scalar(bg[u % 2][:, 1, 0:n], bank(3)[:, 0:n], w["eb1"][:, e * J + 1:e * J + 2], 0.0, ALU.add, ALU.max).then_inc(sem("b_relu1"), 1)

            def b_bias(u):
                e, c = B_STEPS[u]
                dve.wait_ge(sem("b_down"), u + 1)
                if u >= 2:
                    dve.wait_ge(sem("b_back"), u - 1)
                dve.tensor_scalar(by[u % 2][:], bank(4 + u % 2)[:, 0:LEFT], w["eb2"][:, e:e + 1], None, ALU.add).then_inc(sem("b_by"), 1)

            def b_copy(u):
                e, c = B_STEPS[u]
                dve.wait_ge(sem("b_back"), u + 1)
                if e >= 2 and c == 0:
                    dve.wait_ge(sem(f"expert_out{e % 2}"), 16 * (e // 2))
                src = bank(6 + u % 2)[:, 0:2 * P].rearrange("p (r g c) -> p r g c", r=2, g=2)
                if c + 4 <= ET:
                    dve.tensor_copy(yo[e % 2][:, c:c + 4, :].rearrange("p (g r) c -> p r g c", g=2), src).then_inc(sem("b_yo"), 1)
                else:
                    dve.tensor_copy(yo[e % 2][:, c:c + 2, :], src[:, :, 0, :])
                    dve.tensor_copy(yo[e % 2][:, c + 2, :], src[:, 0, 1, :]).then_inc(sem("b_yo"), 1)

            for step in range(1, NU + 4):
                for lag, f in ((1, b_relu1), (2, b_bias), (3, b_copy)):
                    if 0 <= step - lag < NU:
                        f(step - lag)
            dve_second(dve)


def host_inputs(a):
    import numpy as np

    def dup(x):
        return np.concatenate([x, x], axis=0)

    def rows(x, n=P):
        return np.broadcast_to(x.reshape(1, -1), (n, x.size))

    g = 96 // 16
    patches = a["x"].reshape(NB, 3, g, 16, g, 16).transpose(0, 2, 4, 1, 3, 5).reshape(NB * N_IMG, KC * P)
    dim = np.arange(D)
    inv = np.power(np.float32(10000.0), -((dim - dim % 2).astype(np.float32) / np.float32(D))).astype(np.float32)
    angle = np.arange(N_TXT, dtype=np.float32)[:, None] * inv
    pe = np.where(dim % 2 == 0, np.sin(angle), np.cos(angle)).astype(np.float32)
    qkv_w = a["L1_attn_W_qkv"].reshape(D // HC, 3, HC, D)
    qkv_b = a["L1_attn_b_qkv"].reshape(D // HC, 3, HC)
    l1_wq = qkv_w[:, 0].reshape(D, D)
    kv_w = np.concatenate([qkv_w[:, 1].reshape(D, D), qkv_w[:, 2].reshape(D, D)], axis=0)
    kv_b = np.concatenate([qkv_b[:, 1].reshape(D), qkv_b[:, 2].reshape(D)])
    wq, wk = a["L0_attn_wq"], a["L0_attn_wk"]
    head = np.arange(D) // HC
    ex = np.arange(E)

    def hidden(b):
        return b.reshape(E * J, P).T

    def up(w):
        return dup(w.transpose(1, 0, 2).reshape(D, E * F_MOE))

    def down(w):
        return w.reshape(E * J, P, D).transpose(1, 0, 2)

    h = dict(
        table=a["L0_txt_W"], patches=patches.T.reshape(KC, P, NB * N_IMG).transpose(1, 0, 2),
        ids=a["x_txt"].reshape(NB, TXT, P).transpose(2, 0, 1).reshape(P, NB * TXT),
        tok_w=a["L0_tok_W"].T.reshape(KC, P, D).transpose(1, 0, 2), tok_b=a["L0_tok_b"].reshape(D, 1),
        pe=pe.reshape(TXT, P, D).transpose(1, 0, 2),
        norm_g=dup(a["L0_attn_norm_g"].reshape(D, 1)), norm_b=a["L0_attn_norm_b"].reshape(D, 1),
        wq=dup(np.concatenate([wq, wq], 1)), wk=dup(np.concatenate([wk, wk], 1)), wv=dup(a["L0_attn_wv"]),
        bq=dup(a["L0_attn_bq"].reshape(D, 1)), bk=dup(a["L0_attn_bk"].reshape(D, 1)), bv=rows(a["L0_attn_bv"]),
        w1=dup(a["L0_attn_w1"]), b1=a["L0_attn_b1"].reshape(F_ATTN, 1), w2=a["L0_attn_w2"], b2=dup(a["L0_attn_b2"].reshape(D, 1)),
        fg=rows(a["L0_attn_fnorm_g"]), fb=rows(a["L0_attn_fnorm_b"]),
        gw=dup(a["L0_ffn_gate_w"]), gb=rows(a["L0_ffn_gate_b"]),
        ew1=up(a["L0_ffn_w1"]), eb1=hidden(a["L0_ffn_b1"]), ew2=down(a["L0_ffn_w2"]), eb2=dup(a["L0_ffn_b2"].T),
        wkv=dup(kv_w.T), kv_b=rows(kv_b), l1_wq=np.concatenate([l1_wq, qkv_b[:, 0].reshape(D, 1)], 1),
        ak=np.concatenate([rows(a["L1_attn_kln_w"], D), a["L1_attn_kln_b"].reshape(1, D)]),
        av=np.concatenate([rows(a["L1_attn_vln_w"], D), a["L1_attn_vln_b"].reshape(1, D)]),
        wp=a["L1_attn_W_proj"].T, bp=rows(a["L1_attn_b_proj"]),
        wr=dup(a["L1_ffn_Wr"]), br=rows(a["L1_ffn_br"]),
        fw1=up(a["L1_ffn_W1"]), fb1=hidden(a["L1_ffn_b1"]), fw2=down(a["L1_ffn_W2"]), fb2=a["L1_ffn_b2"].reshape(E // 2, P).T,
        fln_g=dup(a["L1_ffn_ln_g"].T), fln_b=a["L1_ffn_ln_b"].T,
        ident=np.eye(P, dtype=np.float32), tri=np.triu(np.ones((P, P), np.float32)),
        diag=np.concatenate([np.eye(D, dtype=np.float32), np.ones((1, D), np.float32)]),
        heads=(head[:, None] == head[None, :]).astype(np.float32) / np.float32(N),
        eye=np.eye(D, D + 1, dtype=np.float32),
        order=np.broadcast_to((E - ex).astype(np.float32), (P, SLOTS, E)),
        base=rows((ex * CP - 1).astype(np.float32)), limit=rows((ex * CP + CAP).astype(np.float32)),
    )
    return {n: np.ascontiguousarray(v) for n, v in h.items()}


def kernel(**inputs):
    import numpy as np
    import concourse.bacc as bacc
    from concourse.bass_utils import run_bass_kernel_spmd

    nc = bacc.Bacc("TRN2", target_bir_lowering=False, num_devices=1)
    arrays = {f"in_{n}": v for n, v in host_inputs({k: np.asarray(v) for k, v in inputs.items()}).items()}
    aps = {n[3:]: nc.dram_tensor(n, list(v.shape), mybir.dt.from_np(v.dtype), kind="ExternalInput").ap() for n, v in arrays.items()}
    out = nc.dram_tensor("out", [NB, N, D], F32, kind="ExternalOutput").ap()
    early_fusion_kernel(nc, aps, out)
    got = run_bass_kernel_spmd(nc, [arrays], core_ids=[0])
    return got.results[0]["out"]
```

```python
from contextlib import ExitStack

import concourse.bass as bass
from concourse import mybir

F32 = mybir.dt.float32
F32R = mybir.dt.float32r
BF16 = mybir.dt.bfloat16
I32 = mybir.dt.int32
ALU = mybir.AluOpType
ACT = mybir.ActivationFunctionType
AX = mybir.AxisListType.X

P = 128
NB, N_IMG, N_TXT, D = 16, 36, 512, 64
N = N_IMG + N_TXT
SLOTS = 5
IMG = 4
TXT = N_TXT // P
NPAD = SLOTS * P
KC = 6
E = 8
F_ATTN = 128
F_MOE = 256
J = F_MOE // P
CAP = -(-5 * NB * N // (4 * E))
ET = -(-CAP // P)
CP = ET * P
DROPPED = 1.0e6
EPS = 1e-5
SCALE = D ** -0.5
HALF = N // 2
LEFT = 2 * P
RIGHT = N - LEFT
HC = 4
FMAX = 3.4028234663852886e38

PER = dict(norm1a=11, norm1b=4, qk_low=3, vals=1, resid=2, norm2a=12, norm2b=5, norm3a=10, norm3b=3, gate=6, place=7,
           mixed=12, weighted=5, norm4=5, kvnorm=3, fold=3, resid2=11, norm5=6, route_a=10, route_b=6)


class Steps:

    def __init__(self, engine, sem, name, b):
        self.engine, self.sem, self.name = engine, sem, name
        self.n, self.end = b * PER[name], (b + 1) * PER[name]

    def __call__(self, ins):
        ins.then_inc(self.sem, 1)
        self.n += 1

    def sync(self):
        self.engine.wait_ge(self.sem, self.n)

    def close(self):
        assert self.n == self.end, (self.name, self.n - self.end + PER[self.name])



class Banks:

    def __init__(self):
        self.reader = {}

    def take(self, pe, banks, sem, value):
        before = {self.reader[k] for k in banks if k in self.reader}
        for s, v in before:
            pe.wait_ge(s, v)
        for k in banks:
            self.reader[k] = (sem, value)


def early_fusion_kernel(nc, i, out):
    with ExitStack() as ctx:
        def sb(name, shape, dt=F32):
            return ctx.enter_context(nc.sbuf_tensor(name, shape, dt))

        def pair(name, shape, dt=F32, depth=2):
            return [sb(f"{name}{k}", shape, dt) for k in range(depth)]

        sems = {}

        def sem(name):
            if name not in sems:
                sems[name] = ctx.enter_context(nc.semaphore(name))
            return sems[name]

        psum = ctx.enter_context(nc.psum_tensor("psum", [P, 8 * 512], F32))

        def bank(k, n=1):
            return psum[:, 512 * k:512 * (k + n)]

        slots_buf = nc.dram_tensor("slots_buf", [E * CP, 2 * D], F32, kind="Internal").ap()
        expert_out = nc.dram_tensor("expert_out", [E * CP, D], F32, kind="Internal").ap()

        H = sb("H", [P, NB, SLOTS, D])
        X = sb("X", [P, NB, SLOTS, D])
        scratch = sb("scratch", [P, 5120])
        early_x = X[:].rearrange("p b s c -> p (b s c)")
        patches = early_x[:, 0:KC * NB * N_IMG].rearrange("p (k n) -> p k n", k=KC)
        ew1 = scratch[:, 0:E * F_MOE]
        fw1 = scratch[:, E * F_MOE:2 * E * F_MOE]
        w = {}
        for name in i:
            if name not in ("table", "patches", "ew1", "fw1"):
                w[name] = sb("w_" + name, list(i[name].shape), i[name].dtype)
        ident = w["ident"]
        tri_b, ones_b = sb("tri_b", [P, P], BF16), sb("ones_b", [P, P], BF16)
        eps_t = sb("eps_t", [P, 2])
        split = {}
        for name, cols in (("wq", P), ("wk", P), ("wv", D), ("w1", F_ATTN), ("gw", E), ("wr", E), ("wkv", 2 * D),
                           ("ew1", E * F_MOE), ("fw1", E * F_MOE)):
            split[name] = (sb(name + "_hi", [P, cols], F32R), sb(name + "_lo", [P, cols], F32R))
        bq, bk, bv = sb("bq", [P, 1]), sb("bk", [P, 1]), sb("bv", [P, D])
        fb1 = sb("fb1", [P, E * J])
        ctr_w, ctr_b = sb("ctr_w", [P, 2 * D // HC]), sb("ctr_b", [P, 2 * D // HC])
        ak, av = sb("ak", [D + 1, D]), sb("av", [D + 1, D])
        img_t = scratch[0:D, 2 * E * F_MOE:2 * E * F_MOE + NB * N_IMG]
        gap = sb("gap", [P, NB, SLOTS, E])
        slot_f, slot_i = sb("slot_f", [P, NB, SLOTS]), sb("slot_i", [P, NB, SLOTS], I32)
        top_w, kept = sb("top_w", [P, NB, SLOTS]), sb("kept", [P, NB, SLOTS])
        carry = sb("carry", [P, E])

        emb = pair("emb", [P, TXT, D])
        stats = sb("stats", [P, SLOTS, 6])
        mv1, mv2, mv3 = (pair(f"mv{k}_", [P, SLOTS, 2]) for k in (1, 2, 3))
        sd1 = pair("sd1_", [P, 2, SLOTS])
        sd2, sd3 = pair("sd2_", [P, SLOTS]), pair("sd3_", [P, SLOTS])
        rs = sb("rs", [P, 2, SLOTS])
        zt, xt, xt3 = (sb(n, [P, SLOTS, D]) for n in ("zt", "xt", "xt3"))
        uu = pair("uu", [P, SLOTS, D])
        hl1, hl2 = pair("hl1_", [P, SLOTS, 2 * D]), pair("hl2_", [P, SLOTS, 2 * D])
        hl3 = pair("hl3_", [P, SLOTS, 2 * D], depth=4)
        xs1, xs2, xs3 = (pair(f"xs{k}_", [P, NPAD], F32R) for k in (1, 2, 3))
        qst = pair("qst", [P, N], F32R)
        kh, kl = pair("kh", [P, NPAD], F32R), pair("kl", [P, NPAD], F32R)
        vv = pair("vv", [P, SLOTS, D])
        prob_t = sb("prob", [P, SLOTS, N])
        prob = [prob_t[:, s, :] for s in range(SLOTS)]
        zeros = sb("zeros", [P, 2 * D])
        ot, yt = pair("ot", [P, RIGHT]), pair("yt", [P, RIGHT])
        rr = pair("rr", [P, SLOTS, D])
        ff = pair("ff", [P, N])
        lg, mx = sb("lg", [P, SLOTS, E]), sb("mx", [P, SLOTS])
        eq, oh1 = sb("eq", [P, SLOTS, E]), sb("oh1", [P, SLOTS, E])
        oh_b = pair("oh_b", [P, SLOTS + 1, E], BF16)
        pl, ov = sb("pl", [P, SLOTS, E]), sb("ov", [P, SLOTS, E])
        def cut(start, k, shape):
            size = shape[0] * shape[1]
            return scratch[:, start + k * size:start + (k + 1) * size].rearrange("p (a c) -> p a c", a=shape[0])

        xl = [cut(0, k, (ET, 2 * D)) for k in range(2)]
        yo = [cut(2 * ET * 2 * D, k, (ET, D)) for k in range(2)]
        by = [scratch[:, 6 * ET * D + k * LEFT:6 * ET * D + (k + 1) * LEFT] for k in range(2)]
        bx = [q[:, 0:512] for q in qst]
        bg = [prob_t[:].rearrange("p s n -> p (s n)")[:, k * J * 512:(k + 1) * J * 512].rearrange("p (j n) -> p j n", j=J) for k in range(2)]

        def bc(a, n):
            return a.unsqueeze(2).to_broadcast([a.shape[0], a.shape[1], n])

        def bs(a, k):
            return a.unsqueeze(1).to_broadcast([a.shape[0], k, a.shape[1]])

        def halves(k):
            return bank(k, 2).rearrange("p (h n) -> p h n", h=2)[:, :, 0:HALF]

        def turned(k):
            return bank(k)[:, 0:4 * D].rearrange("p (r g c) -> p r g c", r=2, g=2)

        def by_pairs(a):
            return a[:, 0:TXT, :].rearrange("p (g r) c -> p r g c", g=2)

        TURN, WIDE, SCORE, MIX, LOW = (0, 1), (2, 3), (4, 5), (6,), (7,)
        LAG = dict(gather=0, norm1=1, cut1=2, qkv=3, attn=4, resid=5, ffn2=6, norm3=7, gate=8, scatter=9)
        STEPS = NB + LAG["scatter"]
        WEIGHTS_STEP = 9

        def at(step, stage):
            b = step - LAG[stage]
            return b if 0 <= b < NB else None

        block = ctx.enter_context(nc.Block())
        EARLY = [n for n in ("ident", "pe", "norm_b", "norm_g", "wq", "wk", "wv", "bq", "bk", "bv", "w1", "b1", "w2", "b2", "fg", "fb", "gw", "gb", "tri", "order", "base", "limit", "tok_b")]
        MIDDLE = ["fln_b", "fln_g", "fb1", "wkv", "kv_b", "ak", "av", "diag"]
        LATE = [n for n in w if n not in EARLY + MIDDLE + ["ids", "tok_w"]]
        EARLY_BY_SP = 12
        EARLY_IN, MIDDLE_IN, LATE_IN = 16 * len(EARLY), 16 * (len(MIDDLE) + 1), 16 * (len(LATE) + 1)
        B_STEPS = [(e, c) for e in range(E) for c in range(0, ET, 4)]
        NU = len(B_STEPS)
        UE = NU // E

        def piece(start, *shape):
            size = 1
            for k in shape:
                size *= k
            v = scratch[:, start:start + size]
            if len(shape) == 2:
                return v.rearrange("p (a c) -> p a c", a=shape[0])
            if len(shape) == 3:
                return v.rearrange("p (a k c) -> p a k c", a=shape[0], k=shape[1])
            return v

        hid = [piece(k * RIGHT, RIGHT) for k in range(8)]
        at0 = 8 * RIGHT
        spare = prob_t[:].rearrange("p s n -> p (s n)")
        kvn = piece(at0, SLOTS, 2, D + 1)
        at0 += SLOTS * 2 * (D + 1)
        acc = (piece(at0, SLOTS, 2, D), spare[:, 0:SLOTS * 2 * D].rearrange("p (s e c) -> p s e c", s=SLOTS, e=2))
        at0 += SLOTS * 2 * D
        tmp = [piece(at0 + k * 3 * P, 3, 2, D) for k in range(2)]
        at0 += 2 * 3 * P
        ssq, ksd, krs = (piece(at0 + k * SLOTS * 32, SLOTS, 32) for k in range(3))
        yg, kvt, ksq, ysb = uu, hl2[0], hl2[1], yt
        gram_s, p1_s, kv_s, a_s, fold_b = ff[0][0:D + 1, 0:D + 1], ff[0][0:D + 1, 128:128 + D], ff[0][0:D, 256:256 + D], ff[0][0:D, 384:384 + D + 1], ff[1][:, 0:D]
        fold_w = (kh[0][:, 0:D], kl[0][:, 0:D])
        pre, gel = vv[0], vv[1]
        good = rr[0]
        above, term = (spare[:, k * SLOTS * D:(k + 1) * SLOTS * D].rearrange("p (s c) -> p s c", s=SLOTS) for k in (2, 3))
        ratio = pair("ratio", [P, SLOTS])
        w8 = pair("w8_", [P, SLOTS, E])
        oh2, ex, qq = sb("oh2_", [P, SLOTS, E]), sb("ex", [P, SLOTS]), sb("qq", [P, SLOTS])
        euler = sb("euler", [P, SLOTS])
        POS = 8
        LAG2 = dict(mixed=0, kv=1, fold=2, norm5=3, moe=4, finish=5)
        STEPS2 = NB + LAG2["finish"]
        PARTS = ((0, LEFT, 0, 2), (LEFT, N, 2, SLOTS))

        def at2(step, stage):
            b = step - LAG2[stage]
            return b if 0 <= b < NB else None

        def up_bank(m):
            return 2 + m % 3

        def unit(n):
            b, k = divmod(n, POS)
            return (b,) + divmod(k, E // 2)

        def wide(k):
            return bank(k, 2)[:, 0:SLOTS * P].rearrange("p (s c) -> p s c", s=SLOTS)

        def groups(a):
            return a.rearrange("p s (g c) -> p s g c", c=HC)

        BY_DVE = 3

        def weighted(engine, b):
            st = Steps(engine, sem("weighted"), "weighted", b)
            engine.wait_ge(sem(f"y_in{b % 2}"), 16 * SLOTS * (b // 2 + 1))
            engine.wait_ge(sem("top_w"), 4)
            y, mask = yg[b % 2], good[:].bitcast(I32)
            if b >= 1:
                engine.wait_ge(sem("mixed"), (b - 1) * PER["mixed"] + 2)
            st(engine.tensor_tensor(y[:], y[:], bc(top_w[:, b, :], D), ALU.mult))
            st.sync()
            st(engine.tensor_scalar(above, y[:], FMAX, 1.0e4, ALU.is_gt, ALU.mult))
            st(engine.tensor_scalar(term, y[:], -FMAX, 1.0e4, ALU.is_lt, ALU.mult))
            st(engine.tensor_scalar(mask, y[:], 0.0, 0.0, ALU.mult, ALU.is_equal))
            st.sync()
            st(engine.tensor_tensor(term, above, term, ALU.subtract))
            st.close()

        def outputs(sp):
            for b in range(NB):
                sp.wait_ge(sem("finish"), 4 * (b + 1))
                sp.dma_start(out[b, N_IMG:N, :].rearrange("(t p) c -> p t c", p=P), H[:, b, 0:TXT, :]).then_inc(sem("out_stored"), 16)
                sp.dma_start(out[b, 0:N_IMG, :], H[0:N_IMG, b, IMG, :]).then_inc(sem("out_stored"), 16)
            sp.wait_ge(sem("out_stored"), 32 * NB)

        def pool_second(pool):
            for k in range(2):
                pool.wait_ge(sem(f"expert_out{k}"), 16 * E // 2)
            pool.memset(euler[:], 2.718281828459045).then_inc(sem("euler"), 1)
            pool.wait_ge(sem("euler"), 1)
            pool.wait_ge(sem("norm2a"), NB * PER["norm2a"])
            pool.wait_ge(sem("norm2b"), NB * PER["norm2b"])

            def gather_y(b):
                if b >= 2:
                    pool.wait_ge(sem("mixed"), (b - 2) * PER["mixed"] + 1)
                for s in range(SLOTS):
                    rows = P if s < TXT else N_IMG
                    pool.indirect_dma_start(yg[b % 2][0:rows, s, :], None, expert_out, bass.IndirectOffsetOnAxis(slot_i[0:rows, b, s:s + 1], 0),
                                            bounds_check=E * CP - 1, oob_is_err=False).then_inc(sem(f"y_in{b % 2}"), 16)

            def input_added(b):
                pool.wait_ge(sem("norm4"), (b + 1) * PER["norm4"])
                pool.tensor_tensor(H[:, b], H[:, b], X[:, b], ALU.add).then_inc(sem("input_added"), 1)

            def finish(b):
                for side, (_, _, s0, s1) in enumerate(PARTS):
                    pool.wait_ge(sem("weigh"), 2 * (POS * b + (side + 1) * E // 2))
                    h = H[:, b, s0:s1, :]
                    for k in range(2):
                        pool.tensor_tensor(h, h, acc[b % 2][:, s0:s1, k, :], ALU.add).then_inc(sem("finish"), 1)
                        pool.wait_ge(sem("finish"), 4 * b + 2 * side + k + 1)

            def second_share(b):
                pool.wait_ge(sem("route_a"), (b + 1) * PER["route_a"])
                if b >= 1:
                    pool.wait_ge(sem("route_b"), b * PER["route_b"])
                pool.tensor_tensor(ex[:], euler[:], mx[:], ALU.pow).then_inc(sem("share"), 1)

            gather_y(0)
            gather_y(1)
            for step in range(STEPS2):
                A, K, W5, M = (at2(step, k) for k in ("mixed", "kv", "norm5", "finish"))
                if A is not None and A >= BY_DVE:
                    weighted(pool, A)
                if M is not None:
                    finish(M)
                if K is not None:
                    input_added(K)
                if W5 is not None:
                    second_share(W5)
                if A is not None and A + 2 < NB:
                    gather_y(A + 2)

        def pe_second(pe):
            NARROW, DOWN, BACK = (5,), (6,), (7,)

            def t4(b):
                banks.take(pe, (0, 1), sem("xs4"), b + 1)
                pe.wait_ge(sem("norm4"), (b + 1) * PER["norm4"])
                turn(pe, hl1[b % 2], 0).then_inc(sem("t4"), 1)

            def kv(b):
                banks.take(pe, (0, 1), sem("kv_b"), b + 1)
                pe.wait_ge(sem("xs4"), b + 1)
                tokens_by(pe, wide(0), xs1[b % 2], split["wkv"], slice(0, 2 * D)).then_inc(sem("kv_prod"), 1)

            def gram(b):
                banks.take(pe, NARROW, sem("gram_s"), b + 1)
                pe.wait_ge(sem("kvnorm"), (b + 1) * PER["kvnorm"])
                for s in range(SLOTS):
                    rows = P if s < TXT else N_IMG
                    last = pe.matmul(bank(5)[0:D + 1, 0:D + 1], kvn[0:rows, s, 0, :], kvn[0:rows, s, 1, :], start=(s == 0), stop=(s == IMG))
                last.then_inc(sem("gram"), 1)

            def gains_k(b):
                banks.take(pe, NARROW, sem("p1_s"), b + 1)
                pe.wait_ge(sem("gram_s"), b + 1)
                pe.matmul(bank(5)[0:D + 1, 0:D], gram_s, ak[:], start=True, stop=True).then_inc(sem("p1"), 1)

            def gains_v(b):
                banks.take(pe, NARROW, sem("kv_s"), b + 1)
                pe.wait_ge(sem("p1_s"), b + 1)
                pe.matmul(bank(5)[0:D, 0:D], p1_s, av[:], start=True, stop=True).then_inc(sem("p2"), 1)

            def by_q(b):
                banks.take(pe, NARROW, sem("a_s"), b + 1)
                pe.wait_ge(sem("kv_s"), b + 1)
                pe.matmul(bank(5)[0:D, 0:D + 1], kv_s, w["l1_wq"][:], start=True, stop=True).then_inc(sem("p3"), 1)

            def by_proj(b):
                banks.take(pe, NARROW, sem("fold"), (b + 1) * PER["fold"])
                pe.wait_ge(sem("a_s"), b + 1)
                for h in range(2):
                    pe.matmul(bank(5)[h * D:(h + 1) * D, 0:D], a_s[:, 0:D], w["wp"][:], start=True, stop=True)
                pe.matmul(bank(5)[:, D:2 * D], a_s[:, D:D + 1].to_broadcast([D, P]), w["wp"][:], start=True, stop=True).then_inc(sem("p4"), 1)

            def proj(b):
                banks.take(pe, (1,), sem("pre"), b + 1)
                pe.wait_ge(sem("fold"), (b + 1) * PER["fold"])
                tokens_by(pe, bank(1)[:, 0:SLOTS * D].rearrange("p (s c) -> p s c", s=SLOTS), xs1[b % 2], fold_w, slice(0, D)).then_inc(sem("proj"), 1)

            def t5(b):
                banks.take(pe, (0, 1), sem("xs5"), b + 1)
                pe.wait_ge(sem("norm5"), (b + 1) * PER["norm5"])
                turn(pe, hl3[b % 2], 0).then_inc(sem("t5"), 1)

            def route(b):
                banks.take(pe, (1,), sem("route_a"), b * PER["route_a"] + 1)
                pe.wait_ge(sem("xs5"), b + 1)
                tokens_by(pe, bank(1)[:, 0:SLOTS * E].rearrange("p (s e) -> p s e", s=SLOTS), xs2[b % 2], split["wr"], slice(0, E)).then_inc(sem("route_prod"), 1)

            def up(n, *tiles):
                b, side, p = unit(n)
                a, z, _, _ = PARTS[side]
                if n % POS == 0 and 0 in tiles:
                    pe.wait_ge(sem("xs5"), b + 1)
                for k in tiles:
                    j, e = k // 2, 2 * p + k % 2
                    m = up_bank(4 * n + k)
                    banks.take(pe, (m,), sem("gelu"), 4 * n + k + 1)
                    two(pe, bank(m)[:, 0:z - a], split["fw1"], xs2[b % 2][:, a:z], slice((e * J + j) * P, (e * J + j + 1) * P)).then_inc(sem("up"), 1)

            def down(n, *tiles):
                b, side, p = unit(n)
                a, z, _, _ = PARTS[side]
                if 0 in tiles:
                    banks.take(pe, DOWN, sem("ysb"), n + 1)
                for j in tiles:
                    pe.wait_ge(sem("gelu"), 4 * n + 2 * j + 2)
                    for h in range(2):
                        last = pe.matmul(bank(6)[h * D:(h + 1) * D, 0:z - a], w["fw2"][:, (2 * p + h) * J + j, :], hid[(4 * n + 2 * j + h) % 8][:, 0:z - a],
                                         start=(j == 0), stop=(j == J - 1))
                if J - 1 in tiles:
                    last.then_inc(sem("down"), 1)

            def back(n):
                b, side, p = unit(n)
                _, _, s0, s1 = PARTS[side]
                banks.take(pe, BACK, sem("weigh"), 2 * n + 1)
                pe.wait_ge(sem("ysb"), n + 1)
                for s in range(s0, s1):
                    rows = P if s < TXT else N_IMG
                    k = (s - s0) * P
                    last = pe.transpose(bank(7)[0:rows, k:k + P], ysb[n % 2][:, k:k + rows], ident[:])
                last.then_inc(sem("back"), 1)

            for step in range(STEPS2):
                K, F, W5 = (at2(step, k) for k in ("kv", "fold", "norm5"))
                for pos in range(POS):
                    n = (step - LAG2["moe"]) * POS + pos
                    now, before = 0 <= n < NB * POS, 0 <= n - 1 < NB * POS
                    if now:
                        up(n, 0, 1)
                    for stage, when, f in PE_ORDER:
                        if when == pos and at2(step, stage) is not None:
                            {"t5": t5, "gram": gram, "gains_k": gains_k, "t4": t4, "gains_v": gains_v, "route": route, "by_q": by_q, "kv": kv,
                             "by_proj": by_proj, "proj": proj}[f](at2(step, stage))
                    if now:
                        up(n, 2)
                    if 0 <= n - 2 < NB * POS:
                        back(n - 2)
                    if now:
                        up(n, 3)
                    if before:
                        down(n - 1, 0, 1)

        def act_second(act):
            def roots4(b):
                act.wait_ge(sem("mixed"), (b + 1) * PER["mixed"])
                if b >= 2:
                    act.wait_ge(sem("norm4"), (b - 2) * PER["norm4"] + 1)
                act.activation(sd2[b % 2][:], mv1[b % 2][:, :, 1], ACT.Sqrt, bias=eps_t[:, 0:1]).then_inc(sem("roots4"), 1)

            def roots_kv(b):
                act.wait_ge(sem("ssq"), b + 1)
                act.activation(ksd, ssq, ACT.Sqrt, scale=1.0 / (HC - 1)).then_inc(sem("roots_kv"), 1)

            def roots5(b):
                act.wait_ge(sem("resid2"), (b + 1) * PER["resid2"])
                if b >= 2:
                    act.wait_ge(sem("norm5"), (b - 1) * PER["norm5"])
                act.activation(sd1[b % 2][:, 0, :], mv2[b % 2][:, :, 1], ACT.Sqrt, bias=eps_t[:, 0:1])
                act.activation(sd1[b % 2][:, 1, :], mv2[b % 2][:, :, 1], ACT.Sqrt, bias=eps_t[:, 1:2], scale=1.0 + EPS).then_inc(sem("roots5"), 1)

            def stack4(b):
                act.wait_ge(sem("t4"), b + 1)
                if b >= 2:
                    act.wait_ge(sem("proj"), b - 1)
                act.activation(xs1[b % 2][:, 0:N], bank(0, 2)[:, 0:N], ACT.Identity).then_inc(sem("xs4"), 1)

            def square(b):
                act.wait_ge(sem("kv_b"), b + 1)
                if b >= 1:
                    act.wait_ge(sem("ssq"), b)
                act.activation(ksq[:], kvt[:], ACT.Square).then_inc(sem("ksq"), 1)

            def gelu_proj(b):
                act.wait_ge(sem("pre"), b + 1)
                if b >= 1:
                    act.wait_ge(sem("resid2"), (b - 1) * PER["resid2"] + 1)
                act.activation(gel[:], pre[:], ACT.Gelu).then_inc(sem("gelu_proj"), 1)

            def stack5(b):
                act.wait_ge(sem("t5"), b + 1)
                if b >= 2:
                    act.wait_ge(sem("up"), 4 * POS * (b - 1))
                act.activation(xs2[b % 2][:, 0:N], bank(0, 2)[:, 0:N], ACT.Identity).then_inc(sem("xs5"), 1)

            def gelu(n, half):
                b, side, p = unit(n)
                a, z, _, _ = PARTS[side]
                for k in (2 * half, 2 * half + 1):
                    j, e = k // 2, 2 * p + k % 2
                    m = 4 * n + k
                    act.wait_ge(sem("up"), m + 1)
                    if m >= 8:
                        act.wait_ge(sem("down"), n - 1)
                    act.activation(hid[m % 8][:, 0:z - a], bank(up_bank(m))[:, 0:z - a], ACT.Gelu, bias=fb1[:, e * J + j:e * J + j + 1]).then_inc(sem("gelu"), 1)

            def add_b2(n):
                b, side, p = unit(n)
                a, z, _, _ = PARTS[side]
                act.wait_ge(sem("down"), n + 1)
                if n >= 2:
                    act.wait_ge(sem("back"), n - 1)
                act.activation(ysb[n % 2][:, 0:z - a], bank(6)[:, 0:z - a], ACT.Identity, bias=w["fb2"][:, p:p + 1]).then_inc(sem("ysb"), 1)

            for k in range(2):
                act.wait_ge(sem(f"expert_out{k}"), 16 * E // 2)
            for step in range(STEPS2):
                for pos in range(POS):
                    n = (step - LAG2["moe"]) * POS + pos
                    if 0 <= n < NB * POS:
                        gelu(n, 0)
                    for stage, when, f in ACT_ORDER:
                        if when == pos and at2(step, stage) is not None:
                            {"roots4": roots4, "roots_kv": roots_kv, "roots5": roots5, "stack4": stack4, "square": square, "gelu_proj": gelu_proj,
                             "stack5": stack5}[f](at2(step, stage))
                    if 0 <= n < NB * POS:
                        gelu(n, 1)
                    if 0 <= n - 1 < NB * POS:
                        add_b2(n - 1)

        def dve_second(dve):
            for k in range(2):
                dve.wait_ge(sem(f"expert_out{k}"), 16 * E // 2)
            dve.memset(kvn[:, :, :, D:D + 1], 1.0).then_inc(sem("kvn_ones"), 1)
            dve.wait_ge(sem("gap_exp"), 1)
            flat = top_w[:].rearrange("p b s -> p (b s)")
            dve.tensor_reduce(flat, gap[:].rearrange("p b s e -> p (b s) e"), AX, ALU.add).then_inc(sem("top_w"), 1)
            dve.tensor_scalar(kept[:], slot_f[:], float(E * CP), None, ALU.is_lt).then_inc(sem("top_w"), 1)
            dve.wait_ge(sem("top_w"), 2)
            dve.reciprocal(top_w[:], top_w[:]).then_inc(sem("top_w"), 1)
            dve.wait_ge(sem("top_w"), 3)
            dve.tensor_tensor(top_w[:], top_w[:], kept[:], ALU.mult).then_inc(sem("top_w"), 1)
            dve.wait_ge(sem("top_w"), 4)

            def mixed(b):
                st = Steps(dve, sem("mixed"), "mixed", b)
                if b < BY_DVE:
                    weighted(dve, b)
                dve.wait_ge(sem("weighted"), (b + 1) * PER["weighted"])
                if b >= 2:
                    dve.wait_ge(sem("roots4"), b - 1)
                st(dve.copy_predicated(term, good[:].bitcast(I32), yg[b % 2][:]))
                st.sync()
                st(dve.tensor_tensor(H[:, b], H[:, b], term, ALU.add))
                st.sync()
                norm_stats(dve, st, H[:, b], mv1[b % 2])
                st.close()

            def norm4(b):
                st = Steps(dve, sem("norm4"), "norm4", b)
                dve.wait_ge(sem("roots4"), b + 1)
                dve.wait_ge(sem("mixed"), (b + 1) * PER["mixed"])
                if b >= 2:
                    dve.wait_ge(sem("t4"), b - 1)
                st(dve.reciprocal(rs[:, 0, :], sd2[b % 2][:]))
                st(dve.tensor_tensor(zt[:], H[:, b], bc(mv1[b % 2][:, :, 0], D), ALU.subtract))
                st.sync()
                st(dve.tensor_tensor(X[:, b], zt[:], bc(rs[:, 0, :], D), ALU.mult))
                st.sync()
                high_low(dve, st, hl1[b % 2], X[:, b])
                st.close()
                st.sync()

            def kv_b(b):
                dve.wait_ge(sem("kv_prod"), b + 1)
                dve.tensor_tensor(kvt[:], wide(0), bs(w["kv_b"][:], SLOTS), ALU.add).then_inc(sem("kv_b"), 1)

            def sum_squares(b):
                dve.wait_ge(sem("ksq"), b + 1)
                if b >= 1:
                    dve.wait_ge(sem("roots_kv"), b)
                dve.tensor_reduce(ssq, groups(ksq[:]), AX, ALU.add).then_inc(sem("ssq"), 1)

            def kvnorm(b):
                st = Steps(dve, sem("kvnorm"), "kvnorm", b)
                dve.wait_ge(sem("roots_kv"), b + 1)
                if b >= 1:
                    dve.wait_ge(sem("gram"), b)
                st(dve.tensor_scalar(krs, ksd, EPS, None, ALU.add))
                st.sync()
                st(dve.reciprocal(krs, krs))
                st.sync()
                for side in range(2):
                    ins = dve.tensor_tensor(kvn[:, :, side, 0:D].rearrange("p s (g c) -> p s g c", c=HC), groups(kvt[:, :, side * D:(side + 1) * D]),
                                            krs[:, :, side * 16:(side + 1) * 16].unsqueeze(3).to_broadcast([P, SLOTS, 16, HC]), ALU.mult)
                st(ins)
                st.close()
                st.sync()

            def copy_out(name, product, dst, src):
                def f(b):
                    dve.wait_ge(sem(product), b + 1)
                    dve.tensor_copy(dst, src).then_inc(sem(name), 1)
                return f

            def own_heads(b):
                dve.wait_ge(sem("p2"), b + 1)
                dve.tensor_tensor(kv_s, bank(5)[0:D, 0:D], w["heads"][:], ALU.mult).then_inc(sem("kv_s"), 1)

            def add_input(b):
                dve.wait_ge(sem("p3"), b + 1)
                dve.tensor_tensor(a_s, bank(5)[0:D, 0:D + 1], w["eye"][:], ALU.add).then_inc(sem("a_s"), 1)

            def fold(b):
                st = Steps(dve, sem("fold"), "fold", b)
                dve.wait_ge(sem("p4"), b + 1)
                if b >= 1:
                    dve.wait_ge(sem("proj"), b)
                st(dve.tensor_copy(fold_w[0], bank(5)[:, 0:D]))
                st.sync()
                st(dve.tensor_tensor(fold_w[1], bank(5)[:, 0:D], fold_w[0].bitcast(F32), ALU.subtract))
                st(dve.tensor_tensor(fold_b, bank(5)[:, D:2 * D], w["bp"][:], ALU.add))
                st.close()
                st.sync()

            def pre_bias(b):
                dve.wait_ge(sem("proj"), b + 1)
                if b >= 1:
                    dve.wait_ge(sem("gelu_proj"), b)
                dve.tensor_tensor(pre[:], bank(1)[:, 0:SLOTS * D].rearrange("p (s c) -> p s c", s=SLOTS), bs(fold_b, SLOTS), ALU.add).then_inc(sem("pre"), 1)

            def resid2(b):
                st = Steps(dve, sem("resid2"), "resid2", b)
                dve.wait_ge(sem("gelu_proj"), b + 1)
                if b >= 2:
                    dve.wait_ge(sem("roots5"), b - 1)
                dve.wait_ge(sem("input_added"), b + 1)
                st(dve.tensor_tensor(H[:, b], H[:, b], gel[:], ALU.add))
                st.sync()
                norm_stats(dve, st, H[:, b], mv2[b % 2])
                st.close()

            def norm5(b):
                st = Steps(dve, sem("norm5"), "norm5", b)
                dve.wait_ge(sem("roots5"), b + 1)
                dve.wait_ge(sem("resid2"), (b + 1) * PER["resid2"])
                if b >= 2:
                    dve.wait_ge(sem("t5"), b - 1)
                st(dve.reciprocal(rs[:], sd1[b % 2][:]))
                st(dve.tensor_tensor(zt[:], H[:, b], bc(mv2[b % 2][:, :, 0], D), ALU.subtract))
                st.sync()
                st(dve.tensor_tensor(ratio[b % 2][:], sd1[b % 2][:, 1, :], rs[:, 0, :], ALU.mult))
                st(dve.tensor_tensor(xt[:], zt[:], bc(rs[:, 1, :], D), ALU.mult))
                st.sync()
                high_low(dve, st, hl3[b % 2], xt[:])
                st.close()
                st.sync()

            def first_of_largest(st, dst):
                st(dve.tensor_reduce(qq[:], eq[:], AX, ALU.max))
                st.sync()
                st(dve.tensor_tensor(dst, eq[:], bc(qq[:], E), ALU.is_equal))
                st.sync()

            def route_a(b):
                st = Steps(dve, sem("route_a"), "route_a", b)
                dve.wait_ge(sem("route_prod"), b + 1)
                if b >= 1:
                    dve.wait_ge(sem("share"), b)
                first = oh1[:]
                st(dve.tensor_tensor(lg[:], bank(1)[:, 0:SLOTS * E].rearrange("p (s e) -> p s e", s=SLOTS), bc(ratio[b % 2][:], E), ALU.mult))
                st.sync()
                st(dve.tensor_tensor(lg[:], lg[:], bs(w["br"][:], SLOTS), ALU.add))
                st.sync()
                st(dve.tensor_reduce(mx[:], lg[:], AX, ALU.max))
                st.sync()
                st(dve.tensor_tensor(lg[:], lg[:], bc(mx[:], E), ALU.subtract))
                st.sync()
                st(dve.scalar_tensor_tensor(out=eq[:], in0=lg[:], scalar=0.0, in1=w["order"][:], op0=ALU.is_ge, op1=ALU.mult))
                st.sync()
                first_of_largest(st, first)
                st(dve.scalar_tensor_tensor(out=lg[:], in0=first, scalar=-1.0e30, in1=lg[:], op0=ALU.mult, op1=ALU.add))
                st.sync()
                st(dve.tensor_reduce(mx[:], lg[:], AX, ALU.max))
                st.sync()
                st(dve.tensor_tensor(lg[:], lg[:], bc(mx[:], E), ALU.subtract))
                st.close()
                st.sync()

            def route_b(b):
                st = Steps(dve, sem("route_b"), "route_b", b)
                dve.wait_ge(sem("share"), b + 1)
                if b >= 2:
                    dve.wait_ge(sem("weigh"), 2 * POS * (b - 1))
                first = oh1[:]
                st(dve.scalar_tensor_tensor(out=eq[:], in0=lg[:], scalar=0.0, in1=w["order"][:], op0=ALU.is_ge, op1=ALU.mult))
                st.sync()
                first_of_largest(st, oh2[:])
                st(dve.tensor_scalar(qq[:], ex[:], 1.0, None, ALU.add))
                st.sync()
                st(dve.reciprocal(qq[:], qq[:]))
                st.sync()
                dve.tensor_tensor(oh2[:], oh2[:], bc(ex[:], E), ALU.mult).then_inc(sem("route_c"), 1)
                dve.wait_ge(sem("route_c"), 2 * b + 1)
                dve.tensor_tensor(oh2[:], oh2[:], first, ALU.add).then_inc(sem("route_c"), 1)
                dve.wait_ge(sem("route_c"), 2 * b + 2)
                st(dve.tensor_tensor(w8[b % 2][:], oh2[:], bc(qq[:], E), ALU.mult))
                st.close()
                st.sync()

            def weigh(n):
                b, side, p = unit(n)
                _, _, s0, s1 = PARTS[side]
                dve.wait_ge(sem("back"), n + 1)
                prod = bank(7)[:, 0:(s1 - s0) * P].rearrange("p (s e c) -> p s e c", s=s1 - s0, e=2)
                share = w8[b % 2][:, s0:s1, 2 * p:2 * p + 2].unsqueeze(3).to_broadcast([P, s1 - s0, 2, D])
                a = acc[b % 2][:, s0:s1]
                if n:
                    dve.wait_ge(sem("weigh"), 2 * n)
                if p == 0:
                    if b >= 2:
                        dve.wait_ge(sem("finish"), 4 * (b - 2) + 2 * (side + 1))
                    dve.tensor_tensor(a, prod, share, ALU.mult).then_inc(sem("weigh"), 2)
                else:
                    t = tmp[n % 2][:, 0:s1 - s0]
                    dve.tensor_tensor(t, prod, share, ALU.mult).then_inc(sem("weigh"), 1)
                    dve.wait_ge(sem("weigh"), 2 * n + 1)
                    dve.tensor_tensor(a, a, t, ALU.add).then_inc(sem("weigh"), 1)

            table = dict(mixed=mixed, norm4=norm4, kv_b=kv_b, sum_squares=sum_squares, kvnorm=kvnorm, own_heads=own_heads, add_input=add_input, fold=fold,
                         pre_bias=pre_bias, resid2=resid2, norm5=norm5, route_a=route_a, route_b=route_b,
                         gram_s=copy_out("gram_s", "gram", gram_s, bank(5)[0:D + 1, 0:D + 1]),
                         p1_s=copy_out("p1_s", "p1", p1_s, bank(5)[0:D + 1, 0:D]))
            for step in range(STEPS2):
                for pos in range(POS):
                    n = (step - LAG2["moe"]) * POS + pos
                    if 0 <= n - 3 < NB * POS:
                        weigh(n - 3)
                    for stage, when, f in DVE_ORDER:
                        if when == pos and at2(step, stage) is not None:
                            table[f](at2(step, stage))

        PE_ORDER = (("norm5", 1, "t5"), ("fold", 2, "gram"), ("norm5", 2, "route"), ("kv", 3, "t4"), ("fold", 3, "gains_k"),
                    ("fold", 4, "gains_v"), ("fold", 5, "by_q"), ("kv", 5, "kv"), ("fold", 6, "by_proj"), ("fold", 7, "proj"))
        ACT_ORDER = (("kv", 0, "roots4"), ("norm5", 0, "roots5"), ("fold", 0, "roots_kv"), ("norm5", 1, "stack5"), ("kv", 4, "stack4"),
                     ("kv", 6, "square"), ("fold", 7, "gelu_proj"))
        DVE_ORDER = (("norm5", 1, "norm5"), ("fold", 1, "kvnorm"), ("kv", 2, "norm4"), ("fold", 3, "gram_s"), ("norm5", 3, "route_a"),
                     ("fold", 3, "p1_s"), ("fold", 4, "own_heads"), ("mixed", 5, "mixed"), ("fold", 5, "add_input"), ("kv", 5, "kv_b"),
                     ("norm5", 6, "route_b"), ("fold", 6, "fold"), ("kv", 6, "sum_squares"), ("fold", 7, "pre_bias"), ("fold", 7, "resid2"))

        def store_expert(sp, e):
            sp.wait_ge(sem("b_yo"), UE * (e + 1))
            sp.dma_start(expert_out[e * CP:(e + 1) * CP, :].rearrange("(p t) c -> p t c", p=P), yo[e % 2][:]).then_inc(sem(f"expert_out{e % 2}"), 16)

        @block.sync
        def _(sp):
            for n in EARLY[:EARLY_BY_SP]:
                sp.dma_start(w[n][:], i[n]).then_inc(sem("early_in"), 16)
            sp.dma_start(fw1, i["fw1"]).then_inc(sem("middle_in"), 16)
            for n in MIDDLE:
                sp.dma_start(w[n][:], i[n]).then_inc(sem("middle_in"), 16)
            sp.dma_start(ew1, i["ew1"]).then_inc(sem("late_in"), 16)
            for n in LATE:
                sp.dma_start(w[n][:], i[n]).then_inc(sem("late_in"), 16)
            sp.wait_ge(sem("zero_set"), 1)
            for e in range(E):
                sp.dma_start(slots_buf[e * CP:(e + 1) * CP, :].rearrange("(p t) c -> p t c", p=P), zeros[:].unsqueeze(1).to_broadcast([P, ET, 2 * D])).then_inc(sem("slots_zeroed"), 16)
            for k in range(4):
                sp.wait_ge(sem(f"scattered{k}"), 16 * SLOTS * NB // 4)
            for e in range(E):
                if e >= 2:
                    sp.wait_ge(sem("b_turn"), UE * (e - 1))
                else:
                    sp.wait_ge(sem("low_w"), 2)
                sp.dma_start(xl[e % 2][:], slots_buf[e * CP:(e + 1) * CP, :].rearrange("(p t) c -> p t c", p=P)).then_inc(sem(f"xl_in{e % 2}"), 16)
                if e >= 2:
                    store_expert(sp, e - 2)
            store_expert(sp, E - 2)
            store_expert(sp, E - 1)
            outputs(sp)

        @block.gpsimd
        def _(pool):
            pool.dma_start(w["ids"][:], i["ids"]).then_inc(sem("ids_in"), 16)
            pool.wait_ge(sem("ids_in"), 16)

            def gather(b):
                if b >= 2:
                    pool.wait_ge(sem("norm1a"), (b - 2) * PER["norm1a"] + 1)
                for t in range(TXT):
                    pool.indirect_dma_start(emb[b % 2][:, t, :], None, i["table"], bass.IndirectOffsetOnAxis(w["ids"][:, b * TXT + t:b * TXT + t + 1], 0)).then_inc(sem(f"gathered{b % 2}"), 16)

            def scatter(b):
                if b == 0:
                    pool.wait_ge(sem("slots_zeroed"), 16 * E)
                pool.wait_ge(sem("place"), (b + 1) * PER["place"])
                for s in range(SLOTS):
                    rows = P if s < TXT else N_IMG
                    pool.indirect_dma_start(slots_buf, bass.IndirectOffsetOnAxis(slot_i[0:rows, b, s:s + 1], 0), hl3[b % 4][0:rows, s, :], None,
                                            bounds_check=E * CP - 1, oob_is_err=False).then_inc(sem(f"scattered{b % 4}"), 16)

            def offset(b):
                if b == 0:
                    pool.wait_ge(sem("prep"), 1)
                pool.wait_ge(sem("norm1b"), (b + 1) * PER["norm1b"])
                pool.tensor_tensor(H[:, b], H[:, b], bs(w["fb"][:], SLOTS), ALU.add).then_inc(sem("offset"), 1)

            def low1(b):
                pool.wait_ge(sem("high1"), b + 1)
                h = hl1[b % 2]
                pool.tensor_tensor(h[:, :, D:2 * D].bitcast(F32R), xt[:], h[:, :, 0:D], ALU.subtract).then_inc(sem("low1"), 1)

            def low3(b):
                pool.wait_ge(sem("high3"), b + 1)
                h = hl3[b % 4]
                pool.tensor_tensor(h[:, :, D:2 * D].bitcast(F32R), xt3[:], h[:, :, 0:D], ALU.subtract).then_inc(sem("low3"), 1)

            for step in range(STEPS):
                if step == WEIGHTS_STEP + 1:
                    pool.wait_ge(sem("high_w"), 2)
                    for name, src in (("ew1", ew1), ("fw1", fw1)):
                        hi, lo = split[name]
                        pool.tensor_tensor(lo[:], src, hi[:].bitcast(F32), ALU.subtract).then_inc(sem("low_w"), 1)
                for stage, f in (("gather", gather), ("cut1", low1), ("qkv", offset), ("scatter", scatter), ("norm3", low3)):
                    if (b := at(step, stage)) is not None:
                        f(b)
            pool_second(pool)

        banks = Banks()

        def turn(pe, src, dst_bank, cols=(2 * D)):
            for s in range(SLOTS):
                rows = P if s < TXT else N_IMG
                last = pe.transpose(bank(dst_bank, 2)[0:cols, s * P:s * P + rows], src[0:rows, s, :], ident[0:rows, 0:rows])
            return last

        def turn_back(pe, src, k):
            pe.transpose(bank(k)[:, 0:P], src[:, 0:P], ident[:])
            pe.transpose(bank(k)[:, P:2 * P], src[:, P:2 * P], ident[:])
            return pe.transpose(bank(k)[0:N_IMG, 2 * P:2 * P + D], src[D:P, LEFT:RIGHT], ident[D:P, D:P])

        def two(pe, dst, parts, rhs, cols=slice(None)):
            pe.matmul(dst, parts[0][:, cols], rhs, start=True, stop=False)
            return pe.matmul(dst, parts[1][:, cols], rhs, start=False, stop=True)

        def tokens_by(pe, dst, stack, parts, cols):
            for s in range(SLOTS):
                pe.matmul(dst[:, s, :], stack[:, s * P:(s + 1) * P], parts[0][:, cols], start=True, stop=False)
                last = pe.matmul(dst[:, s, :], stack[:, s * P:(s + 1) * P], parts[1][:, cols], start=False, stop=True)
            return last

        @block.tensor
        def _(pe):
            pe.wait_ge(sem("patches_in"), 32)
            for h in range(2):
                for k in range(KC):
                    last = pe.matmul(bank(h)[0:D, 0:NB * N_IMG // 2], w["tok_w"][:, k, :], patches[:, k, h * NB * N_IMG // 2:(h + 1) * NB * N_IMG // 2],
                                     start=(k == 0), stop=(k == KC - 1))
            last.then_inc(sem("patch_prod"), 1)
            pe.wait_ge(sem("early_in"), EARLY_IN)
            pe.wait_ge(sem("zero_set"), 1)
            pe.matmul(bank(7)[:, 0:1], w["wq"][0:D, :], w["norm_b"][:], start=True, stop=True)
            pe.matmul(bank(7)[:, 1:2], w["wk"][0:D, :], w["norm_b"][:], start=True, stop=True)
            pe.matmul(bank(7)[:, 64:64 + D], w["norm_b"][:].to_broadcast([D, P]), w["wv"][0:D, :], start=True, stop=True).then_inc(sem("bias_prod"), 1)
            pe.wait_ge(sem("img_t"), 2)
            for b in range(NB):
                last = pe.transpose(bank(2 + b // 8)[0:N_IMG, (b % 8) * D:(b % 8 + 1) * D], img_t[:, b * N_IMG:(b + 1) * N_IMG], ident[0:D, 0:D])
            last.then_inc(sem("img_turn"), 1)
            pe.wait_ge(sem("prep"), 1)

            def t1(b):
                banks.take(pe, TURN, sem("xs1"), b + 1)
                pe.wait_ge(sem("low1"), b + 1)
                turn(pe, hl1[b % 2], 0).then_inc(sem("t1"), 1)

            def q_or_k(b, name):
                banks.take(pe, WIDE, sem("qk_low"), b * PER["qk_low"] + (1 if name == "wq" else 3))
                pe.wait_ge(sem("xs1"), b + 1)
                for h in range(2):
                    last = two(pe, bank(2 + h)[:, 0:HALF], split[name], xs1[b % 2][:, h * HALF:(h + 1) * HALF])
                last.then_inc(sem("qk_prod"), 1)

            def q(b):
                q_or_k(b, "wq")

            def k(b):
                q_or_k(b, "wk")

            def v(b):
                banks.take(pe, LOW, sem("vals"), b + 1)
                pe.wait_ge(sem("xs1"), b + 1)
                tokens_by(pe, bank(7)[:, 0:SLOTS * D].rearrange("p (s c) -> p s c", s=SLOTS), xs1[b % 2], split["wv"], slice(0, D)).then_inc(sem("v_prod"), 1)

            spans = ((0, LEFT), (LEFT, N))

            def scores(b, s):
                if s == 0:
                    pe.wait_ge(sem("qk_low"), (b + 1) * PER["qk_low"])
                for h, (a, z) in enumerate(spans):
                    n = b * 2 * SLOTS + 2 * s + h
                    banks.take(pe, (SCORE[h],), sem("relu"), n + 1)
                    dst = bank(SCORE[h])[:, 0:z - a]
                    pe.matmul(dst, kh[b % 2][:, s * P:(s + 1) * P], qst[b % 2][:, a:z], start=True, stop=False)
                    pe.matmul(dst, kl[b % 2][:, s * P:(s + 1) * P], qst[b % 2][:, a:z], start=False, stop=True).then_inc(sem("scores"), 1)

            def attend(b, s):
                if b == 0 and s == 0:
                    pe.wait_ge(sem("moe_bias"), 1)
                if s == 0:
                    banks.take(pe, MIX, sem("ot"), b + 1)
                    pe.wait_ge(sem("vals"), (b + 1) * PER["vals"])
                pe.wait_ge(sem("relu"), b * 2 * SLOTS + 2 * s + 2)
                for h, (a, z) in enumerate(spans):
                    last = pe.matmul(bank(6)[h * D:(h + 1) * D, 0:z - a], vv[b % 2][:, s, :], prob[s][:, a:z], start=(s == 0), stop=(s == SLOTS - 1))
                last.then_inc(sem("attend"), 1)

            def o_turn(b):
                banks.take(pe, TURN, sem("resid"), b * PER["resid"] + 2)
                pe.wait_ge(sem("ot"), b + 1)
                turn_back(pe, ot[b % 2], 0).then_inc(sem("o_turn"), 1)

            def t2(b):
                banks.take(pe, TURN, sem("xs2"), b + 1)
                pe.wait_ge(sem("low2"), b + 1)
                turn(pe, hl2[b % 2], 0).then_inc(sem("t2"), 1)

            def ffn1(b):
                banks.take(pe, WIDE, sem("ff"), b + 1)
                pe.wait_ge(sem("xs2"), b + 1)
                for h in range(2):
                    last = two(pe, bank(2 + h)[:, 0:HALF], split["w1"], xs2[b % 2][:, h * HALF:(h + 1) * HALF])
                last.then_inc(sem("ffn1"), 1)

            def ffn2(b):
                banks.take(pe, LOW, sem("yt"), b + 1)
                pe.wait_ge(sem("ff"), b + 1)
                for h, (a, z) in enumerate(spans):
                    last = pe.matmul(bank(7)[h * D:(h + 1) * D, 0:z - a], w["w2"][:], ff[b % 2][:, a:z], start=True, stop=True)
                last.then_inc(sem("ffn2"), 1)

            def y_turn(b):
                banks.take(pe, TURN, sem("norm2a"), b * PER["norm2a"] + 2)
                pe.wait_ge(sem("yt"), b + 1)
                turn_back(pe, yt[b % 2], 0).then_inc(sem("y_turn"), 1)

            def t3(b):
                banks.take(pe, TURN, sem("xs3"), b + 1)
                pe.wait_ge(sem("low3"), b + 1)
                turn(pe, hl3[b % 4], 0).then_inc(sem("t3"), 1)

            def gate(b):
                banks.take(pe, LOW, sem("gate"), b * PER["gate"] + 1)
                pe.wait_ge(sem("xs3"), b + 1)
                tokens_by(pe, bank(7)[:, 0:SLOTS * E].rearrange("p (s e) -> p s e", s=SLOTS), xs3[b % 2], split["gw"], slice(0, E)).then_inc(sem("gate_prod"), 1)

            def count(b):
                banks.take(pe, LOW, sem("place"), b * PER["place"] + 2)
                pe.wait_ge(sem("gate"), (b + 1) * PER["gate"])
                o, dst = oh_b[b % 2], bank(7)[:, 0:(SLOTS + 1) * E].rearrange("p (s e) -> p s e", e=E)
                last = pe.matmul(dst, tri_b[:], o[:], start=True, stop=False, skip_group_check=True)
                for s in (IMG, 0, 1, 2, 3):
                    rows = N_IMG if s == IMG else P
                    first = 0 if s == IMG else s + 1
                    if first < TXT:
                        pe.matmul(dst[:, first:TXT, :], ones_b[0:rows, :], bs(o[0:rows, s, :], TXT - first), start=False, stop=False, skip_group_check=True)
                    last = pe.matmul(dst[:, SLOTS, :], ones_b[0:rows, :], o[0:rows, s, :], start=False, stop=(s == 3), skip_group_check=True)
                last.then_inc(sem("count"), 1)

            def moe_bias(pe):
                pe.wait_ge(sem("middle_in"), MIDDLE_IN)
                for k in range(E * J):
                    last = pe.matmul(bank(6)[:, k:1 + k], fw1[0:D, k * P:(k + 1) * P], w["fln_b"][:, k // J:k // J + 1], start=True, stop=True)
                last.then_inc(sem("moe_bias_prod"), 1)

            for step in range(STEPS):
                if step == LAG["attn"] - 1:
                    moe_bias(pe)
                A, Q, R, Y, G = (at(step, k) for k in ("attn", "qkv", "resid", "ffn2", "gate"))
                for s in range(SLOTS + 1):
                    if A is not None and s < SLOTS:
                        scores(A, s)
                    for stage, when, f in ((Q, 0, t1), (Y, 0, ffn2), (R, 1, o_turn), (Q, 1, q), (G, 1, t3), (Y, 2, y_turn), (G, 2, gate),
                                           (Q, 2, k), (R, 3, t2), (Q, 3, v), (G, 4, count), (R, 5, ffn1)):
                        if when == s and stage is not None:
                            f(stage)
                    if A is not None and s >= 1:
                        attend(A, s - 1)

            def b_turn(u):
                e, c = B_STEPS[u]
                if c == 0:
                    pe.wait_ge(sem(f"xl_in{e % 2}"), 16 * (e // 2 + 1))
                banks.take(pe, (u % 2,), sem("b_bx"), u + 1)
                for k, t in enumerate(range(c, min(c + 4, ET))):
                    last = pe.transpose(bank(u % 2)[:, k * P:(k + 1) * P], xl[e % 2][:, t, :], ident[:])
                last.then_inc(sem("b_turn"), 1)

            def b_up(u):
                e, c = B_STEPS[u]
                n = P * (min(c + 4, ET) - c)
                pe.wait_ge(sem("b_bx"), u + 1)
                for j in range(J):
                    banks.take(pe, (2 + j,), sem(f"b_relu{j}"), u + 1)
                    two(pe, bank(2 + j)[:, 0:n], split["ew1"], bx[u % 2][:, 0:n], slice((e * J + j) * P, (e * J + j + 1) * P)).then_inc(sem(f"b_up{j}"), 1)

            def b_down(u):
                e, c = B_STEPS[u]
                n = P * (min(c + 4, ET) - c)
                banks.take(pe, (4 + u % 2,), sem("b_by"), u + 1)
                for j in range(J):
                    pe.wait_ge(sem(f"b_relu{j}"), u + 1)
                    for h, (a, z) in enumerate(((0, LEFT), (LEFT, n))):
                        last = pe.matmul(bank(4 + u % 2)[h * D:(h + 1) * D, 0:z - a], w["ew2"][:, e * J + j, :], bg[u % 2][:, j, a:z], start=(j == 0), stop=(j == J - 1))
                last.then_inc(sem("b_down"), 1)

            def b_back(u):
                e, c = B_STEPS[u]
                banks.take(pe, (6 + u % 2,), sem("b_yo"), u + 1)
                pe.wait_ge(sem("b_by"), u + 1)
                pe.transpose(bank(6 + u % 2)[:, 0:P], by[u % 2][:, 0:P], ident[:])
                rows = P if c + 4 <= ET else D
                pe.transpose(bank(6 + u % 2)[:, P:P + rows], by[u % 2][0:rows, P:2 * P], ident[0:rows, 0:rows]).then_inc(sem("b_back"), 1)

            pe.wait_ge(sem("low_w"), 2)
            for step in range(NU + 3):
                for lag, f in ((0, b_turn), (1, b_up), (2, b_down), (3, b_back)):
                    if 0 <= step - lag < NU:
                        f(step - lag)
            pe_second(pe)

        @block.scalar
        def _(act):
            act.dma_start(w["tok_w"][:], i["tok_w"]).then_inc(sem("patches_in"), 16)
            act.dma_start(patches, i["patches"]).then_inc(sem("patches_in"), 16)
            for n in EARLY[EARLY_BY_SP:]:
                act.dma_start(w[n][:], i[n]).then_inc(sem("early_in"), 16)
            act.wait_ge(sem("early_in"), EARLY_IN)
            act.wait_ge(sem("zero_set"), 1)
            act.wait_ge(sem("patch_prod"), 1)
            for h in range(2):
                act.activation(img_t[:, h * NB * N_IMG // 2:(h + 1) * NB * N_IMG // 2], bank(h)[0:D, 0:NB * N_IMG // 2], ACT.Identity, bias=w["tok_b"][:]).then_inc(sem("img_t"), 1)
            act.wait_ge(sem("img_turn"), 1)
            act.activation(H[0:N_IMG, :, IMG, :], bank(2, 2)[0:N_IMG, :].rearrange("p (b c) -> p b c", b=NB), ACT.Identity).then_inc(sem("img_h"), 1)
            act.wait_ge(sem("prep"), 1)

            def roots1(b):
                act.wait_ge(sem("norm1a"), (b + 1) * PER["norm1a"])
                if b >= 2:
                    act.wait_ge(sem("norm1b"), (b - 2) * PER["norm1b"] + 1)
                act.activation(sd1[b % 2][:, 0, :], mv1[b % 2][:, :, 1], ACT.Sqrt, bias=eps_t[:, 0:1])
                act.activation(sd1[b % 2][:, 1, :], mv1[b % 2][:, :, 1], ACT.Sqrt, bias=eps_t[:, 1:2], scale=1.0 + EPS).then_inc(sem("roots1"), 1)

            def high1(b):
                act.wait_ge(sem("norm1b"), (b + 1) * PER["norm1b"])
                if b >= 2:
                    act.wait_ge(sem("t1"), b - 1)
                act.activation(hl1[b % 2][:, :, 0:D].bitcast(F32R), xt[:], ACT.Identity).then_inc(sem("high1"), 1)

            def high2(b):
                act.wait_ge(sem("resid"), (b + 1) * PER["resid"])
                if b >= 2:
                    act.wait_ge(sem("t2"), b - 1)
                act.activation(hl2[b % 2][:, :, 0:D].bitcast(F32R), rr[b % 2][:], ACT.Identity).then_inc(sem("high2"), 1)

            def high3(b):
                act.wait_ge(sem("norm3b"), (b + 1) * PER["norm3b"])
                if b >= 4:
                    act.wait_ge(sem(f"scattered{b % 4}"), 16 * SLOTS * (b // 4))
                    act.wait_ge(sem("t3"), b - 3)
                act.activation(hl3[b % 4][:, :, 0:D].bitcast(F32R), xt3[:], ACT.Identity).then_inc(sem("high3"), 1)

            def stack1(b):
                act.wait_ge(sem("t1"), b + 1)
                if b >= 2:
                    act.wait_ge(sem("v_prod"), b - 1)
                    act.wait_ge(sem("qk_prod"), 2 * (b - 1))
                act.activation(xs1[b % 2][:, 0:N], bank(0, 2)[:, 0:N], ACT.Identity).then_inc(sem("xs1"), 1)

            def q_high(b):
                act.wait_ge(sem("qk_prod"), 2 * b + 1)
                if b >= 2:
                    act.wait_ge(sem("scores"), (b - 1) * 2 * SLOTS)
                act.activation(qst[b % 2][:].rearrange("p (h n) -> p h n", h=2), halves(2), ACT.Identity, bias=bq[:]).then_inc(sem("qk_high"), 1)

            def k_high(b):
                act.wait_ge(sem("qk_prod"), 2 * b + 2)
                act.activation(kh[b % 2][:, 0:N].rearrange("p (h n) -> p h n", h=2), halves(2), ACT.Identity, bias=bk[:]).then_inc(sem("qk_high"), 1)

            def relu(b, s):
                for h, (a, z) in enumerate(((0, LEFT), (LEFT, N))):
                    act.wait_ge(sem("scores"), b * 2 * SLOTS + 2 * s + h + 1)
                    if b >= 1 and h == 0:
                        act.wait_ge(sem("attend"), (b - 1) * SLOTS + s + 1)
                    act.activation(prob[s][:, a:z], bank(SCORE[h])[:, 0:z - a], ACT.Relu, scale=SCALE).then_inc(sem("relu"), 1)

            def o_copy(b):
                act.wait_ge(sem("attend"), (b + 1) * SLOTS)
                if b >= 2:
                    act.wait_ge(sem("o_turn"), b - 1)
                act.activation(ot[b % 2][:], bank(6)[:, 0:RIGHT], ACT.Identity).then_inc(sem("ot"), 1)

            def stack2(b):
                act.wait_ge(sem("t2"), b + 1)
                if b >= 2:
                    act.wait_ge(sem("ffn1"), b - 1)
                act.activation(xs2[b % 2][:, 0:N], bank(0, 2)[:, 0:N], ACT.Identity).then_inc(sem("xs2"), 1)

            def ffn_relu(b):
                act.wait_ge(sem("ffn1"), b + 1)
                if b >= 2:
                    act.wait_ge(sem("ffn2"), b - 1)
                act.activation(ff[b % 2][:].rearrange("p (h n) -> p h n", h=2), halves(2), ACT.Relu, bias=w["b1"][:]).then_inc(sem("ff"), 1)

            def y_copy(b):
                act.wait_ge(sem("ffn2"), b + 1)
                if b >= 2:
                    act.wait_ge(sem("y_turn"), b - 1)
                act.activation(yt[b % 2][:], bank(7)[:, 0:RIGHT], ACT.Identity, bias=w["b2"][:]).then_inc(sem("yt"), 1)

            def root(b, which, mv, sd):
                act.wait_ge(sem(which + "a"), (b + 1) * PER[which + "a"])
                if b >= 2:
                    act.wait_ge(sem(which + "b"), (b - 2) * PER[which + "b"] + 1)
                act.activation(sd[b % 2][:], mv[b % 2][:, :, 1], ACT.Sqrt, bias=eps_t[:, 0:1]).then_inc(sem("root_" + which), 1)

            def root2(b):
                root(b, "norm2", mv2, sd2)

            def root3(b):
                root(b, "norm3", mv3, sd3)

            def stack3(b):
                act.wait_ge(sem("t3"), b + 1)
                if b >= 2:
                    act.wait_ge(sem("gate_prod"), b - 1)
                act.activation(xs3[b % 2][:, 0:N], bank(0, 2)[:, 0:N], ACT.Identity).then_inc(sem("xs3"), 1)

            for step in range(STEPS):
                if step == WEIGHTS_STEP:
                    act.wait_ge(sem("late_in"), LATE_IN)
                    act.activation(split["ew1"][0][:], ew1, ACT.Identity).then_inc(sem("high_w"), 1)
                    act.wait_ge(sem("gains_in"), 1)
                    act.activation(split["fw1"][0][:], fw1, ACT.Identity).then_inc(sem("high_w"), 1)
                A, Q, R, Y, N3, G, N1, C1 = (at(step, k) for k in ("attn", "qkv", "resid", "ffn2", "norm3", "gate", "norm1", "cut1"))
                for s in range(SLOTS + 1):
                    if A is not None and s < SLOTS:
                        relu(A, s)
                    for stage, when, f in ((Q, 0, stack1), (Y, 0, y_copy), (Q, 0, q_high), (R, 1, high2), (G, 1, stack3), (C1, 2, high1),
                                           (N3, 2, root3), (N1, 2, roots1), (Q, 3, k_high), (R, 3, stack2), (Y, 4, root2), (N3, 5, high3),
                                           (A, 5, o_copy), (R, 5, ffn_relu)):
                        if when == s and stage is not None:
                            f(stage)

            act.wait_ge(sem("place"), NB * PER["place"])
            act.activation(gap[:], gap[:], ACT.Exp).then_inc(sem("gap_exp"), 1)

            def b_stack(u):
                e, c = B_STEPS[u]
                n = P * (min(c + 4, ET) - c)
                act.wait_ge(sem("b_turn"), u + 1)
                if u >= 2:
                    act.wait_ge(sem("b_up1"), u - 1)
                act.activation(bx[u % 2][:, 0:n], bank(u % 2)[:, 0:n], ACT.Identity).then_inc(sem("b_bx"), 1)

            def b_relu0(u):
                e, c = B_STEPS[u]
                n = P * (min(c + 4, ET) - c)
                act.wait_ge(sem("b_up0"), u + 1)
                if u >= 2:
                    act.wait_ge(sem("b_down"), u - 1)
                act.activation(bg[u % 2][:, 0, 0:n], bank(2)[:, 0:n], ACT.Relu, bias=w["eb1"][:, e * J:e * J + 1]).then_inc(sem("b_relu0"), 1)

            for step in range(NU + 1):
                for lag, f in ((0, b_stack), (1, b_relu0)):
                    if 0 <= step - lag < NU:
                        f(step - lag)
            act_second(act)

        def norm_stats(dve, st, src, mv):
            for s in range(SLOTS):
                st(dve.bn_stats(stats[:, s, :], src[:, s, :]))
            st.sync()
            for s in range(SLOTS):
                st(dve.bn_aggr(mv[:, s, :], stats[:, s, :]))

        def high_low(dve, st, dst, src):
            st(dve.tensor_copy(dst[:, :, 0:D].bitcast(F32R), src))
            st.sync()
            st(dve.tensor_tensor(dst[:, :, D:2 * D].bitcast(F32R), src, dst[:, :, 0:D], ALU.subtract))

        @block.vector
        def _(dve):
            n_prep = [0]

            def step_of(ins):
                ins.then_inc(sem("prep_steps"), 1)
                n_prep[0] += 1

            def sync():
                dve.wait_ge(sem("prep_steps"), n_prep[0])

            step_of(dve.memset(zeros[:], 0.0))
            step_of(dve.memset(H[:, :, IMG, :], 0.0))
            for tile in (*hl1, *hl2, *hl3, *rr, *uu):
                step_of(dve.memset(tile[:, IMG, :], 0.0))
            for tile in (*oh_b, bank(4, 4)):
                step_of(dve.memset(tile[:], 0.0))
            for tile in (*xs1, *xs2, *xs3, *kh, *kl):
                step_of(dve.memset(tile[:, N:NPAD].bitcast(F32), 0.0))
            step_of(dve.memset(eps_t[:, 0:1], EPS))
            step_of(dve.memset(eps_t[:, 1:2], EPS * EPS))
            step_of(dve.memset(ones_b[:], 1.0))
            sync()
            dve.engine_nop().then_inc(sem("zero_set"), 1)
            dve.wait_ge(sem("early_in"), EARLY_IN)
            step_of(dve.tensor_copy(tri_b[:], w["tri"][:]))
            step_of(dve.tensor_copy(carry[:], w["base"][:]))
            dve.wait_ge(sem("bias_prod"), 1)
            step_of(dve.tensor_tensor(bq[:], bank(7)[:, 0:1], w["bq"][:], ALU.add))
            step_of(dve.tensor_tensor(bk[:], bank(7)[:, 1:2], w["bk"][:], ALU.add))
            step_of(dve.tensor_tensor(bv[:], bank(7)[:, 64:64 + D], w["bv"][:], ALU.add))
            for n in ("wq", "wk", "wv"):
                step_of(dve.tensor_scalar(w[n][:], w[n][:], w["norm_g"][:, 0:1], None, ALU.mult))
            sync()

            def split_weights(sources):
                for n, src in sources:
                    step_of(dve.tensor_copy(split[n][0][:], src))
                sync()
                for n, src in sources:
                    step_of(dve.tensor_tensor(split[n][1][:], src, split[n][0][:].bitcast(F32), ALU.subtract))
                sync()

            split_weights([(n, w[n][:]) for n in ("wq", "wk", "wv", "w1", "gw")])
            dve.wait_ge(sem("img_h"), 1)
            dve.engine_nop().then_inc(sem("prep"), 1)

            def late_weights(part):
                if part == 0:
                    dve.wait_ge(sem("middle_in"), MIDDLE_IN)
                    dve.wait_ge(sem("moe_bias_prod"), 1)
                    kv = w["wkv"][:].rearrange("p (g c) -> p g c", c=HC)
                    kb = w["kv_b"][:].rearrange("p (g c) -> p g c", c=HC)
                    step_of(dve.tensor_reduce(ctr_w[:], kv, AX, ALU.add))
                    step_of(dve.tensor_reduce(ctr_b[:], kb, AX, ALU.add))
                    step_of(dve.tensor_tensor(fb1[:], bank(6)[:, 0:E * J], w["fb1"][:], ALU.add))
                    dve.engine_nop().then_inc(sem("moe_bias"), 1)
                    for e in range(E):
                        cols = fw1[:, e * F_MOE:(e + 1) * F_MOE]
                        step_of(dve.tensor_scalar(cols, cols, w["fln_g"][:, e:e + 1], None, ALU.mult))
                    step_of(dve.tensor_tensor(ak[:], w["ak"][:], w["diag"][:], ALU.mult))
                    step_of(dve.tensor_tensor(av[:], w["av"][:], w["diag"][:], ALU.mult))
                    sync()
                    step_of(dve.tensor_scalar(ctr_w[:], ctr_w[:], 1.0 / HC, None, ALU.mult))
                    step_of(dve.tensor_scalar(ctr_b[:], ctr_b[:], 1.0 / HC, None, ALU.mult))
                    sync()
                    step_of(dve.tensor_tensor(kv, kv, bc(ctr_w[:], HC), ALU.subtract))
                    step_of(dve.tensor_tensor(kb, kb, bc(ctr_b[:], HC), ALU.subtract))
                    sync()
                    dve.engine_nop().then_inc(sem("gains_in"), 1)
                elif part == 1:
                    dve.wait_ge(sem("late_in"), LATE_IN)
                    split_weights([("wr", w["wr"][:]), ("wkv", w["wkv"][:])])

            def norm1a(b):
                st = Steps(dve, sem("norm1a"), "norm1a", b)
                dve.wait_ge(sem(f"gathered{b % 2}"), 16 * TXT * (b // 2 + 1))
                if b >= 2:
                    dve.wait_ge(sem("roots1"), b - 1)
                st(dve.tensor_tensor(H[:, b, 0:TXT, :], emb[b % 2][:], w["pe"][:], ALU.add))
                st.sync()
                norm_stats(dve, st, H[:, b], mv1[b % 2])
                st.close()

            def norm1b(b):
                st = Steps(dve, sem("norm1b"), "norm1b", b)
                dve.wait_ge(sem("roots1"), b + 1)
                dve.wait_ge(sem("norm1a"), (b + 1) * PER["norm1a"])
                if b >= 1:
                    dve.wait_ge(sem("low1"), b)
                st(dve.reciprocal(rs[:], sd1[b % 2][:]))
                st(dve.tensor_tensor(zt[:], H[:, b], bc(mv1[b % 2][:, :, 0], D), ALU.subtract))
                st.sync()
                st(dve.tensor_tensor(xt[:], zt[:], bc(rs[:, 1, :], D), ALU.mult))
                st(dve.tensor_tensor(X[:, b], zt[:], bc(rs[:, 0, :], D), ALU.mult))
                st.sync()
                st.close()
                st.sync()

            def q_low(b):
                dve.wait_ge(sem("qk_high"), 2 * b + 1)
                lo = qst[b % 2][D:P, :].rearrange("p (h n) -> p h n", h=2)
                dve.scalar_tensor_tensor(out=lo, in0=halves(2)[D:P], scalar=bq[D:P, 0:1], in1=lo.bitcast(F32), op0=ALU.add, op1=ALU.subtract).then_inc(sem("qk_low"), 1)

            def k_low(b):
                dve.wait_ge(sem("qk_high"), 2 * b + 2)
                hi = kh[b % 2][:, 0:N].rearrange("p (h n) -> p h n", h=2)
                lo = kl[b % 2][:, 0:N].rearrange("p (h n) -> p h n", h=2)
                dve.scalar_tensor_tensor(out=lo, in0=halves(2), scalar=bk[:, 0:1], in1=hi.bitcast(F32), op0=ALU.add, op1=ALU.subtract).then_inc(sem("qk_low"), 2)

            def vals(b):
                dve.wait_ge(sem("v_prod"), b + 1)
                if b >= 2:
                    dve.wait_ge(sem("attend"), (b - 1) * SLOTS)
                dve.tensor_tensor(vv[b % 2][:], bank(7)[:, 0:SLOTS * D].rearrange("p (s c) -> p s c", s=SLOTS), bs(bv[:], SLOTS), ALU.add).then_inc(sem("vals"), 1)

            def resid(b):
                st = Steps(dve, sem("resid"), "resid", b)
                dve.wait_ge(sem("o_turn"), b + 1)
                r = rr[b % 2]
                st(dve.tensor_tensor(by_pairs(r), turned(0), by_pairs(X[:, b]), ALU.add))
                st(dve.tensor_tensor(r[0:N_IMG, IMG, :], bank(0)[0:N_IMG, 2 * P:2 * P + D], X[0:N_IMG, b, IMG, :], ALU.add))
                st.close()

            def low2(b):
                dve.wait_ge(sem("high2"), b + 1)
                h = hl2[b % 2]
                dve.tensor_tensor(h[:, :, D:2 * D].bitcast(F32R), rr[b % 2][:], h[:, :, 0:D], ALU.subtract).then_inc(sem("low2"), 1)

            def norm2a(b):
                st = Steps(dve, sem("norm2a"), "norm2a", b)
                dve.wait_ge(sem("y_turn"), b + 1)
                if b >= 2:
                    dve.wait_ge(sem("root_norm2"), b - 1)
                r, u = rr[b % 2], uu[b % 2]
                st(dve.tensor_tensor(by_pairs(u), turned(0), by_pairs(r), ALU.add))
                st(dve.tensor_tensor(u[0:N_IMG, IMG, :], bank(0)[0:N_IMG, 2 * P:2 * P + D], r[0:N_IMG, IMG, :], ALU.add))
                st.sync()
                norm_stats(dve, st, u[:], mv2[b % 2])
                st.close()

            def norm2b(b):
                st = Steps(dve, sem("norm2b"), "norm2b", b)
                dve.wait_ge(sem("root_norm2"), b + 1)
                dve.wait_ge(sem("norm2a"), (b + 1) * PER["norm2a"])
                st(dve.reciprocal(rs[:, 0, :], sd2[b % 2][:]))
                st(dve.tensor_tensor(zt[:], uu[b % 2][:], bc(mv2[b % 2][:, :, 0], D), ALU.subtract))
                st.sync()
                st(dve.tensor_tensor(zt[:], zt[:], bc(rs[:, 0, :], D), ALU.mult))
                st.sync()
                st(dve.tensor_tensor(zt[:], zt[:], bs(w["fg"][:], SLOTS), ALU.mult))
                st.sync()
                dve.wait_ge(sem("offset"), b + 1)
                st(dve.tensor_tensor(H[:, b], H[:, b], zt[:], ALU.add))
                st.close()
                st.sync()

            def norm3a(b):
                st = Steps(dve, sem("norm3a"), "norm3a", b)
                if b >= 2:
                    dve.wait_ge(sem("root_norm3"), b - 1)
                norm_stats(dve, st, H[:, b], mv3[b % 2])
                st.close()

            def norm3b(b):
                st = Steps(dve, sem("norm3b"), "norm3b", b)
                dve.wait_ge(sem("root_norm3"), b + 1)
                dve.wait_ge(sem("norm3a"), (b + 1) * PER["norm3a"])
                if b >= 1:
                    dve.wait_ge(sem("low3"), b)
                st(dve.reciprocal(rs[:, 0, :], sd3[b % 2][:]))
                st(dve.tensor_tensor(zt[:], H[:, b], bc(mv3[b % 2][:, :, 0], D), ALU.subtract))
                st.sync()
                st(dve.tensor_tensor(xt3[:], zt[:], bc(rs[:, 0, :], D), ALU.mult))
                st.close()
                st.sync()

            def gate(b):
                st = Steps(dve, sem("gate"), "gate", b)
                dve.wait_ge(sem("gate_prod"), b + 1)
                if b >= 2:
                    dve.wait_ge(sem("count"), b - 1)
                st(dve.tensor_tensor(lg[:], bank(7)[:, 0:SLOTS * E].rearrange("p (s e) -> p s e", s=SLOTS), bs(w["gb"][:], SLOTS), ALU.add))
                st.sync()
                st(dve.tensor_reduce(mx[:], lg[:], AX, ALU.max))
                st.sync()
                st(dve.tensor_tensor(gap[:, b], lg[:], bc(mx[:], E), ALU.subtract))
                st.sync()
                st(dve.scalar_tensor_tensor(out=eq[:], in0=gap[:, b], scalar=0.0, in1=w["order"][:], op0=ALU.is_ge, op1=ALU.mult))
                st.sync()
                st(dve.tensor_reduce(mx[:], eq[:], AX, ALU.max))
                st.sync()
                st(dve.tensor_tensor(oh_b[b % 2][:, 0:SLOTS, :], eq[:], bc(mx[:], E), ALU.is_equal))
                st.close()

            def place(b):
                st = Steps(dve, sem("place"), "place", b)
                dve.wait_ge(sem("count"), b + 1)
                c = bank(7)[:, 0:(SLOTS + 1) * E].rearrange("p (s e) -> p s e", e=E)
                st(dve.tensor_tensor(pl[:], c[:, 0:SLOTS, :], bs(carry[:], SLOTS), ALU.add))
                st.sync()
                st(dve.tensor_tensor(carry[:], c[:, SLOTS, :], carry[:], ALU.add))
                st(dve.tensor_tensor(ov[:], pl[:], bs(w["limit"][:], SLOTS), ALU.is_ge))
                st.sync()
                st(dve.scalar_tensor_tensor(out=pl[:], in0=ov[:], scalar=DROPPED, in1=pl[:], op0=ALU.mult, op1=ALU.add))
                st.sync()
                st(dve.tensor_tensor(pl[:], pl[:], oh_b[b % 2][:, 0:SLOTS, :], ALU.mult))
                st.sync()
                st(dve.tensor_reduce(slot_f[:, b, :], pl[:], AX, ALU.add))
                st.sync()
                st(dve.tensor_copy(slot_i[:, b, :], slot_f[:, b, :]))
                st.close()
                st.sync()

            for step in range(STEPS):
                late_weights(step - 3)
                N1, Q, R, Y, N3, G = (at(step, k) for k in ("norm1", "qkv", "resid", "ffn2", "norm3", "gate"))
                for stage, f in ((R, resid), (Q, q_low), (R, low2), (N1, norm1a), (Y, norm2a), (G, gate), (N3, norm3b), (Q, k_low), (Q, vals),
                                 (N1, norm1b), (Y, norm2b), (G, place), (Y, norm3a)):
                    if stage is not None:
                        f(stage)

            def b_relu1(u):
                e, c = B_STEPS[u]
                n = P * (min(c + 4, ET) - c)
                dve.wait_ge(sem("b_up1"), u + 1)
                if u >= 2:
                    dve.wait_ge(sem("b_down"), u - 1)
                dve.tensor_scalar(bg[u % 2][:, 1, 0:n], bank(3)[:, 0:n], w["eb1"][:, e * J + 1:e * J + 2], 0.0, ALU.add, ALU.max).then_inc(sem("b_relu1"), 1)

            def b_bias(u):
                e, c = B_STEPS[u]
                dve.wait_ge(sem("b_down"), u + 1)
                if u >= 2:
                    dve.wait_ge(sem("b_back"), u - 1)
                dve.tensor_scalar(by[u % 2][:], bank(4 + u % 2)[:, 0:LEFT], w["eb2"][:, e:e + 1], None, ALU.add).then_inc(sem("b_by"), 1)

            def b_copy(u):
                e, c = B_STEPS[u]
                dve.wait_ge(sem("b_back"), u + 1)
                if e >= 2 and c == 0:
                    dve.wait_ge(sem(f"expert_out{e % 2}"), 16 * (e // 2))
                src = bank(6 + u % 2)[:, 0:2 * P].rearrange("p (r g c) -> p r g c", r=2, g=2)
                if c + 4 <= ET:
                    dve.tensor_copy(yo[e % 2][:, c:c + 4, :].rearrange("p (g r) c -> p r g c", g=2), src).then_inc(sem("b_yo"), 1)
                else:
                    dve.tensor_copy(yo[e % 2][:, c:c + 2, :], src[:, :, 0, :])
                    dve.tensor_copy(yo[e % 2][:, c + 2, :], src[:, 0, 1, :]).then_inc(sem("b_yo"), 1)

            for step in range(1, NU + 4):
                for lag, f in ((1, b_relu1), (2, b_bias), (3, b_copy)):
                    if 0 <= step - lag < NU:
                        f(step - lag)
            dve_second(dve)


def host_inputs(a):
    import numpy as np

    def dup(x):
        return np.concatenate([x, x], axis=0)

    def rows(x, n=P):
        return np.broadcast_to(x.reshape(1, -1), (n, x.size))

    g = 96 // 16
    patches = a["x"].reshape(NB, 3, g, 16, g, 16).transpose(0, 2, 4, 1, 3, 5).reshape(NB * N_IMG, KC * P)
    dim = np.arange(D)
    inv = np.power(np.float32(10000.0), -((dim - dim % 2).astype(np.float32) / np.float32(D))).astype(np.float32)
    angle = np.arange(N_TXT, dtype=np.float32)[:, None] * inv
    pe = np.where(dim % 2 == 0, np.sin(angle), np.cos(angle)).astype(np.float32)
    qkv_w = a["L1_attn_W_qkv"].reshape(D // HC, 3, HC, D)
    qkv_b = a["L1_attn_b_qkv"].reshape(D // HC, 3, HC)
    l1_wq = qkv_w[:, 0].reshape(D, D)
    kv_w = np.concatenate([qkv_w[:, 1].reshape(D, D), qkv_w[:, 2].reshape(D, D)], axis=0)
    kv_b = np.concatenate([qkv_b[:, 1].reshape(D), qkv_b[:, 2].reshape(D)])
    wq, wk = a["L0_attn_wq"], a["L0_attn_wk"]
    head = np.arange(D) // HC
    ex = np.arange(E)

    def hidden(b):
        return b.reshape(E * J, P).T

    def up(w):
        return dup(w.transpose(1, 0, 2).reshape(D, E * F_MOE))

    def down(w):
        return w.reshape(E * J, P, D).transpose(1, 0, 2)

    h = dict(
        table=a["L0_txt_W"], patches=patches.T.reshape(KC, P, NB * N_IMG).transpose(1, 0, 2),
        ids=a["x_txt"].reshape(NB, TXT, P).transpose(2, 0, 1).reshape(P, NB * TXT),
        tok_w=a["L0_tok_W"].T.reshape(KC, P, D).transpose(1, 0, 2), tok_b=a["L0_tok_b"].reshape(D, 1),
        pe=pe.reshape(TXT, P, D).transpose(1, 0, 2),
        norm_g=dup(a["L0_attn_norm_g"].reshape(D, 1)), norm_b=a["L0_attn_norm_b"].reshape(D, 1),
        wq=dup(np.concatenate([wq, wq], 1)), wk=dup(np.concatenate([wk, wk], 1)), wv=dup(a["L0_attn_wv"]),
        bq=dup(a["L0_attn_bq"].reshape(D, 1)), bk=dup(a["L0_attn_bk"].reshape(D, 1)), bv=rows(a["L0_attn_bv"]),
        w1=dup(a["L0_attn_w1"]), b1=a["L0_attn_b1"].reshape(F_ATTN, 1), w2=a["L0_attn_w2"], b2=dup(a["L0_attn_b2"].reshape(D, 1)),
        fg=rows(a["L0_attn_fnorm_g"]), fb=rows(a["L0_attn_fnorm_b"]),
        gw=dup(a["L0_ffn_gate_w"]), gb=rows(a["L0_ffn_gate_b"]),
        ew1=up(a["L0_ffn_w1"]), eb1=hidden(a["L0_ffn_b1"]), ew2=down(a["L0_ffn_w2"]), eb2=dup(a["L0_ffn_b2"].T),
        wkv=dup(kv_w.T), kv_b=rows(kv_b), l1_wq=np.concatenate([l1_wq, qkv_b[:, 0].reshape(D, 1)], 1),
        ak=np.concatenate([rows(a["L1_attn_kln_w"], D), a["L1_attn_kln_b"].reshape(1, D)]),
        av=np.concatenate([rows(a["L1_attn_vln_w"], D), a["L1_attn_vln_b"].reshape(1, D)]),
        wp=a["L1_attn_W_proj"].T, bp=rows(a["L1_attn_b_proj"]),
        wr=dup(a["L1_ffn_Wr"]), br=rows(a["L1_ffn_br"]),
        fw1=up(a["L1_ffn_W1"]), fb1=hidden(a["L1_ffn_b1"]), fw2=down(a["L1_ffn_W2"]), fb2=a["L1_ffn_b2"].reshape(E // 2, P).T,
        fln_g=dup(a["L1_ffn_ln_g"].T), fln_b=a["L1_ffn_ln_b"].T,
        ident=np.eye(P, dtype=np.float32), tri=np.triu(np.ones((P, P), np.float32)),
        diag=np.concatenate([np.eye(D, dtype=np.float32), np.ones((1, D), np.float32)]),
        heads=(head[:, None] == head[None, :]).astype(np.float32) / np.float32(N),
        eye=np.eye(D, D + 1, dtype=np.float32),
        order=np.broadcast_to((E - ex).astype(np.float32), (P, SLOTS, E)),
        base=rows((ex * CP - 1).astype(np.float32)), limit=rows((ex * CP + CAP).astype(np.float32)),
    )
    return {n: np.ascontiguousarray(v) for n, v in h.items()}


def kernel(**inputs):
    import numpy as np
    import concourse.bacc as bacc
    from concourse.bass_utils import run_bass_kernel_spmd

    nc = bacc.Bacc("TRN2", target_bir_lowering=False, num_devices=1)
    arrays = {f"in_{n}": v for n, v in host_inputs({k: np.asarray(v) for k, v in inputs.items()}).items()}
    aps = {n[3:]: nc.dram_tensor(n, list(v.shape), mybir.dt.from_np(v.dtype), kind="ExternalInput").ap() for n, v in arrays.items()}
    out = nc.dram_tensor("out", [NB, N, D], F32, kind="ExternalOutput").ap()
    early_fusion_kernel(nc, aps, out)
    got = run_bass_kernel_spmd(nc, [arrays], core_ids=[0])
    return got.results[0]["out"]
```
